# Optimizing a Trainium2 kernel written in Bass

```python
import numpy as np
import jax
import jax.numpy as jnp

def _softmax(x, axis=-1):
    return jax.nn.softmax(x, axis=axis)

def _gelu(x):
    return jax.nn.gelu(x, approximate=True)

def _silu(x):
    return jax.nn.silu(x)

def _sigmoid(x):
    return jax.nn.sigmoid(x)

def _layernorm(x, axis=-1, eps=1e-05):
    m = jnp.mean(x, axis=axis, keepdims=True)
    v = jnp.var(x, axis=axis, keepdims=True)
    return (x - m) / jnp.sqrt(v + eps)

def _scatter_add(tgt, idx, src, axis=0):
    return tgt.at[idx].add(src)

def _segment_sum(src, seg, n):
    return jax.ops.segment_sum(src, seg, n)
kernel_name = 'mk_flamingo_gated_d1_seqx_r4_cb415b'

def setup_inputs(seed: int=0):
    np.random.seed(seed)
    _w = jnp.asarray

    def _rec_inputs():
        import jax
        import jax.numpy as jnp
        _rk = jax.random.key(seed)
        x = -0.0003929 + 0.9999 * jax.random.normal(jax.random.fold_in(_rk, 1), (4, 512, 256), jnp.float32)
        _lenS = 512 - jax.random.randint(jax.random.fold_in(_rk, 7), (4,), 0, max(1, 512 // 4) + 1, jnp.int32)
        _lenS2 = 512 - jax.random.randint(jax.random.fold_in(_rk, 8), (4,), 0, max(1, 512 // 4) + 1, jnp.int32)
        _ctx_1024P = jax.random.normal(jax.random.fold_in(_rk, 11), (4, 16, 256), jnp.float32)
        _ctx_1024c = jax.random.dirichlet(jax.random.fold_in(_rk, 511), 0.3 * jnp.ones((16,), jnp.float32), (4, 512))
        _ctx_1024t = jnp.einsum('bsk,bkd->bsd', _ctx_1024c, _ctx_1024P)
        _ctx_1024t = _ctx_1024t * jax.lax.rsqrt(jnp.mean(jnp.square(_ctx_1024t)) + 1e-12) * 0.953939
        ctx_1024 = 2.81802e-05 + 1.00001 * (_ctx_1024t + 0.3 * jax.random.normal(jax.random.fold_in(_rk, 611), (4, 512, 256), jnp.float32))
        _validS = jnp.arange(512)[None, :] < _lenS[:, None]
        _validS2 = jnp.arange(512)[None, :] < _lenS2[:, None]
        _causal = jnp.tril(jnp.ones((512, 512), dtype=bool))
        mask_BxS2_bf1 = jnp.ones((4, 512), dtype=bool)
        _g = jax.random.normal(jax.random.fold_in(_rk, 9001), (2, 1), jnp.float32)
        _g = jnp.sign(_g) * jnp.maximum(jnp.abs(_g), 1.0) + (_g == 0) * 1.0
        g_xattn = _g[0]
        g_ffn = _g[1]
        return (x, ctx_1024, mask_BxS2_bf1, g_xattn, g_ffn)
    x, ctx_1024, mask_BxS2_bf1, g_xattn, g_ffn = _rec_inputs()

    def _L0_xattn_setup():
        import jax, jax.numpy as jnp
        import numpy as np
        B, N, D_MODEL, H, W = (4, 1024, 256, 16, 64)
        D_K = D_MODEL // H

        def _look_around(x, pad_value):
            pad_width = [(0, 0), (1, 0), (0, 0)] + [(0, 0)] * (x.ndim - 3)
            padded = jnp.pad(x, pad_width, constant_values=pad_value)
            return jnp.concatenate([padded[:, :-1], padded[:, 1:]], axis=2)

        def _local_attention(q, k, v, mask):
            b, h, n, d = q.shape
            nw = n // W
            scale = d ** (-0.5)
            bq = (q * scale).reshape(b * h, nw, W, d)
            bk = _look_around(k.reshape(b * h, nw, W, d), 0.0)
            bv = _look_around(v.reshape(b * h, nw, W, d), 0.0)
            pos = jnp.arange(n).reshape(1, nw, W)
            bq_t = pos
            bq_k = _look_around(pos, -1)
            causal = bq_t[..., :, None] >= bq_k[..., None, :]
            valid = (bq_k != -1)[..., None, :]
            kmask = _look_around(mask.reshape(b, nw, W), False)
            kmask = jnp.repeat(kmask, h, axis=0)[:, :, None, :]
            full_mask = causal & valid & kmask
            sim = jnp.einsum('bnid,bnjd->bnij', bq, bk)
            sim = jnp.where(full_mask, sim, jnp.finfo(sim.dtype).min)
            attn = jax.nn.softmax(sim, axis=-1)
            out = jnp.einsum('bnij,bnjd->bnid', attn, bv)
            return out.reshape(b, h, n, d)
        key = jax.random.key(seed)
        ks = jax.random.split(key, 12)
        mk = lambda k, shape: jax.random.normal(k, shape, dtype=jnp.float32)
        inp = {'query': mk(ks[0], (B, N, D_MODEL)), 'key': mk(ks[1], (B, N, D_MODEL)), 'value': mk(ks[2], (B, N, D_MODEL)), 'mask': jnp.ones((B, N), dtype=bool)}
        scale = 0.02
        for i, nm in enumerate(['q', 'k', 'v', 'o']):
            inp[f'W_{nm}'] = mk(ks[3 + 2 * i], (D_MODEL, D_MODEL)) * scale
            inp[f'b_{nm}'] = jnp.zeros((D_MODEL,), dtype=jnp.float32)
        return inp
    _L0_xattn_all = _L0_xattn_setup()
    _L0_xattn_in = {k: v for k, v in _L0_xattn_all.items() if k in ('W_q', 'b_q', 'W_k', 'b_k', 'W_v', 'b_v', 'W_o', 'b_o')}
    del _L0_xattn_all

    def _L0_ffn_setup():
        import jax, jax.numpy as jnp
        import numpy as np
        import math
        D_MODEL = 256
        N_EXPERTS = 16
        D_FF = 1024
        CAP_FACTOR = 1.25
        MIN_CAPACITY = 4

        def _capacity(num_tokens, num_experts):
            cap = math.floor(CAP_FACTOR * num_tokens / num_experts)
            cap += cap % 2
            return max(cap, MIN_CAPACITY)

        def _top1_router(gate_logits, capacity):
            s, e = gate_logits.shape
            probs = jax.nn.softmax(gate_logits, axis=-1)
            top1 = jnp.argmax(gate_logits, axis=-1)
            mask = jax.nn.one_hot(top1, e, dtype=jnp.int32)
            ranks = jnp.cumsum(mask, axis=0) - 1
            mask = mask * (ranks < capacity).astype(jnp.int32)
            rank1 = jnp.sum(mask * ranks, axis=-1)
            ranks_oh = jax.nn.one_hot(rank1, capacity, dtype=probs.dtype)
            weight = mask.astype(probs.dtype) * probs
            combine_weights = weight[:, :, None] * ranks_oh[:, None, :]
            sec_mask = combine_weights > 0
            return (combine_weights, sec_mask)
        key = jax.random.key(seed)
        k1, k2, k3, k4 = jax.random.split(key, 4)
        x = jax.random.normal(k1, (4, 512, D_MODEL), dtype=jnp.float32)
        gate_w = jax.random.normal(k2, (N_EXPERTS, D_MODEL), dtype=jnp.float32) * math.sqrt(0.1 / D_MODEL)
        w1 = jax.random.normal(k3, (N_EXPERTS, D_MODEL, D_FF), dtype=jnp.float32) * (1.0 / math.sqrt(D_MODEL))
        w2 = jax.random.normal(k4, (N_EXPERTS, D_FF, D_MODEL), dtype=jnp.float32) * (1.0 / math.sqrt(D_FF))
        return {'x': x, 'gate_w': gate_w, 'w1': w1, 'w2': w2}
    _L0_ffn_all = _L0_ffn_setup()
    _L0_ffn_in = {k: v for k, v in _L0_ffn_all.items() if k in ('gate_w', 'w1', 'w2')}
    del _L0_ffn_all
    return {'x': x, 'ctx_1024': ctx_1024, 'mask_BxS2_bf1': mask_BxS2_bf1, 'g_xattn': g_xattn, 'g_ffn': g_ffn, 'L0_xattn_W_q': _L0_xattn_in['W_q'], 'L0_xattn_b_q': _L0_xattn_in['b_q'], 'L0_xattn_W_k': _L0_xattn_in['W_k'], 'L0_xattn_b_k': _L0_xattn_in['b_k'], 'L0_xattn_W_v': _L0_xattn_in['W_v'], 'L0_xattn_b_v': _L0_xattn_in['b_v'], 'L0_xattn_W_o': _L0_xattn_in['W_o'], 'L0_xattn_b_o': _L0_xattn_in['b_o'], 'L0_ffn_gate_w': _L0_ffn_in['gate_w'], 'L0_ffn_w1': _L0_ffn_in['w1'], 'L0_ffn_w2': _L0_ffn_in['w2']}

def reference(x, ctx_1024, mask_BxS2_bf1, g_xattn, g_ffn, L0_xattn_W_q, L0_xattn_b_q, L0_xattn_W_k, L0_xattn_b_k, L0_xattn_W_v, L0_xattn_b_v, L0_xattn_W_o, L0_xattn_b_o, L0_ffn_gate_w, L0_ffn_w1, L0_ffn_w2):
    import jax
    import jax.numpy as jnp

    def _L0_xattn_ref(query, key, value, mask, W_q, b_q, W_k, b_k, W_v, b_v, W_o, b_o):
        import jax, jax.numpy as jnp
        import numpy as np
        B, N, D_MODEL, H, W = (4, 1024, 256, 16, 64)
        D_K = D_MODEL // H

        def _look_around(x, pad_value):
            pad_width = [(0, 0), (1, 0), (0, 0)] + [(0, 0)] * (x.ndim - 3)
            padded = jnp.pad(x, pad_width, constant_values=pad_value)
            return jnp.concatenate([padded[:, :-1], padded[:, 1:]], axis=2)

        def _local_attention(q, k, v, mask):
            b, h, n, d = q.shape
            nw = n // W
            scale = d ** (-0.5)
            bq = (q * scale).reshape(b * h, nw, W, d)
            bk = _look_around(k.reshape(b * h, nw, W, d), 0.0)
            bv = _look_around(v.reshape(b * h, nw, W, d), 0.0)
            pos = jnp.arange(n).reshape(1, nw, W)
            bq_t = pos
            bq_k = _look_around(pos, -1)
            causal = bq_t[..., :, None] >= bq_k[..., None, :]
            valid = (bq_k != -1)[..., None, :]
            kmask = _look_around(mask.reshape(b, nw, W), False)
            kmask = jnp.repeat(kmask, h, axis=0)[:, :, None, :]
            full_mask = causal & valid & kmask
            sim = jnp.einsum('bnid,bnjd->bnij', bq, bk)
            sim = jnp.where(full_mask, sim, jnp.finfo(sim.dtype).min)
            attn = jax.nn.softmax(sim, axis=-1)
            out = jnp.einsum('bnij,bnjd->bnid', attn, bv)
            return out.reshape(b, h, n, d)
        b, n, _ = query.shape

        def proj(x, Wm, bias):
            return (x @ Wm.T + bias).reshape(b, n, H, D_K).transpose(0, 2, 1, 3)
        q = proj(query, W_q, b_q)
        k = proj(key, W_k, b_k)
        v = proj(value, W_v, b_v)
        x = _local_attention(q, k, v, mask)
        x = x.transpose(0, 2, 1, 3).reshape(b, n, H * D_K)
        return x @ W_o.T + b_o

    def _L0_ffn_ref(x, gate_w, w1, w2):
        import jax, jax.numpy as jnp
        import numpy as np
        import math
        D_MODEL = 256
        N_EXPERTS = 16
        D_FF = 1024
        CAP_FACTOR = 1.25
        MIN_CAPACITY = 4

        def _capacity(num_tokens, num_experts):
            cap = math.floor(CAP_FACTOR * num_tokens / num_experts)
            cap += cap % 2
            return max(cap, MIN_CAPACITY)

        def _top1_router(gate_logits, capacity):
            s, e = gate_logits.shape
            probs = jax.nn.softmax(gate_logits, axis=-1)
            top1 = jnp.argmax(gate_logits, axis=-1)
            mask = jax.nn.one_hot(top1, e, dtype=jnp.int32)
            ranks = jnp.cumsum(mask, axis=0) - 1
            mask = mask * (ranks < capacity).astype(jnp.int32)
            rank1 = jnp.sum(mask * ranks, axis=-1)
            ranks_oh = jax.nn.one_hot(rank1, capacity, dtype=probs.dtype)
            weight = mask.astype(probs.dtype) * probs
            combine_weights = weight[:, :, None] * ranks_oh[:, None, :]
            sec_mask = combine_weights > 0
            return (combine_weights, sec_mask)
        tokens = x.reshape(-1, D_MODEL)
        s = tokens.shape[0]
        capacity = _capacity(s, N_EXPERTS)
        gate_logits = tokens.astype(jnp.float32) @ gate_w.T
        combine_weights, sec_mask = _top1_router(gate_logits, capacity)
        dispatch = jnp.einsum('sec,sd->ecd', sec_mask.astype(tokens.dtype), tokens)
        h = jax.nn.gelu(jnp.einsum('ecd,edf->ecf', dispatch, w1))
        expert_out = jnp.einsum('ecf,efd->ecd', h, w2)
        out = jnp.einsum('sec,ecd->sd', combine_weights.astype(tokens.dtype), expert_out)
        return out.reshape(x.shape)
    x = x + jnp.tanh(g_xattn[0]) * _L0_xattn_ref(_layernorm(x, axis=-1), ctx_1024, ctx_1024, mask_BxS2_bf1, L0_xattn_W_q, L0_xattn_b_q, L0_xattn_W_k, L0_xattn_b_k, L0_xattn_W_v, L0_xattn_b_v, L0_xattn_W_o, L0_xattn_b_o)
    x = x + jnp.tanh(g_ffn[0]) * _L0_ffn_ref(_layernorm(x, axis=-1), L0_ffn_gate_w, L0_ffn_w1, L0_ffn_w2)
    return x

_drawn_inputs = setup_inputs


def setup_inputs(seed=0):
    import zlib

    import numpy as np

    out = dict(_drawn_inputs(seed))
    spreads = {'L0_xattn_b_q': (0.0, 0.8),
     'L0_xattn_b_k': (0.0, 0.8),
     'L0_xattn_b_v': (0.0, 0.294),
     'L0_xattn_b_o': (0.0, 0.1)}
    factors = {'L0_xattn_W_q': 8.0, 'L0_xattn_W_k': 8.0}
    for name, (base, spread) in spreads.items():
        noise = np.random.default_rng([zlib.crc32(name.encode()), seed]).standard_normal(out[name].shape)
        drawn = base * np.exp(spread * noise) if base else spread * noise
        out[name] = jnp.asarray(drawn.astype(out[name].dtype))
    for name, factor in factors.items():
        out[name] = (out[name] * factor).astype(out[name].dtype)
    return out
```

```python
from contextlib import ExitStack

import concourse.bass as bass
from concourse import mybir

F32 = mybir.dt.float32
BF16 = mybir.dt.bfloat16
U32 = mybir.dt.uint32
ALU = mybir.AluOpType
ACT = mybir.ActivationFunctionType
AX = mybir.AxisListType

P = 128
WINDOW = 64
HEADS = 16
EPS = 1e-5
MASKED = 1e30
DROPPED = 8192.0
NO_TOKEN = 1048576.0


def capacity(tokens, experts):
    cap = int(1.25 * tokens // experts)
    return max(cap + cap % 2, 4)


def flamingo_kernel(nc, x, ctx_in, mask, g_xattn, g_ffn, W_q, b_q, W_k, b_k, W_v, b_v, W_o, b_o,
                    gate_w, w1, w2, out):
    B, S, D = x.shape
    E, _, F = w1.shape
    T = S // P
    KD = D // P
    KF = F // P
    NW = S // WINDOW
    HD = D // HEADS
    HG = P // HD
    PAIRS = HG // 2
    CAP = capacity(B * S, E)
    SR = CAP // 2
    ROW = 2 * D + 2
    UNITS = 2 * KD * 4
    CHUNKS = UNITS // 4
    assert (T, KD, NW, HG, UNITS) == (4, 2, 8, 8, 16) and CAP % 32 == 0 and E % 2 == 0

    out_rows = out.rearrange("b s d -> (b s) d")
    queue = nc.dram_tensor("expert_queue", (E * CAP, ROW), F32, kind="Internal").ap()

    es = ExitStack()
    with es:
        def sb(name, shape, dt=F32):
            return es.enter_context(nc.sbuf_tensor(name, shape, dt))

        def sem(name):
            return es.enter_context(nc.semaphore(name))

        ident = sb("ident", [P, P])
        head_mask = sb("head_mask", [P, HG])
        parity_mask = sb("parity_mask", [P, 2])
        causal = sb("causal", [P, 2 * WINDOW], BF16)
        before = sb("before", [P, P], BF16)
        ones = sb("ones", [P, P], BF16)
        countdown = sb("countdown", [P, T, E])
        token_no = sb("token_no", [P, B * T])
        minus_half = sb("minus_half", [P, T])
        eps = sb("eps", [P, T])
        empty_row = sb("empty_row", [P, ROW])
        gates = sb("gates", [P, 2])
        tanh_g = sb("tanh_g", [P, 2])
        bias_qk_raw = sb("bias_qk_raw", [P, 2, KD])
        bias_q = sb("bias_q", [P, KD])
        bias_v = sb("bias_v", [P, D])
        bias_o = sb("bias_o", [P, D])
        bias_og = sb("bias_og", [P, D])
        mask_u8 = sb("mask_u8", [P, B, S], mask.dtype)
        key_valid = sb("key_valid", [P, B, WINDOW + S], BF16)
        mask_add = sb("mask_add", [P, B, 2, NW // 2, 2 * WINDOW], BF16)
        mask_now = sb("mask_now", [P, 2, NW // 2, 2 * WINDOW], BF16)
        w_raw = sb("w_raw", [P, 4, KD, D])
        gate_raw = sb("gate_raw", [E, D])
        wT = sb("wT", [P, 4, KD, D])
        gateT = sb("gateT", [P, KD, E])
        x_all = sb("x_all", [P, B, T, D])
        ctx_rows = sb("ctx_rows", [P, T, D])
        xn = sb("xn", [P, T, D])
        stats = sb("stats", [P, T, 6])
        mean_var = sb("mean_var", [P, T, 2])
        var_eps = sb("var_eps", [P, T])
        rstd = sb("rstd", [P, T])
        xnT = sb("xnT", [P, KD, S])
        ctxT = sb("ctxT", [P, KD, S])
        qT = sb("qT", [P, KD, S])
        kT = sb("kT", [P, KD, WINDOW + S])
        q_heads = sb("q_heads", [P, KD, NW, HG, WINDOW])
        v = sb("v", [P, T, D])
        v_shift = sb("v_shift", [P, T, D])
        NP_ = 4
        probs = sb("probs", [P, NP_, PAIRS, 2 * WINDOW])
        low = sb("low", [P, NP_, PAIRS])
        total = sb("total", [P, NP_, PAIRS])
        r_total = sb("r_total", [P, NP_, PAIRS])
        probsT = sb("probsT", [P, 2, PAIRS, 2 * WINDOW])
        attT = sb("attT", [P, KD, S])
        rows = sb("rows", [P, T, ROW])
        stats2 = sb("stats2", [P, T, 6])
        mean_var2 = sb("mean_var2", [P, T, 2])
        var_eps2 = sb("var_eps2", [P, T])
        rstd2 = sb("rstd2", [P, T])
        x1nT = sb("x1nT", [P, KD, S])
        top = sb("top", [P, T])
        lowered = sb("lowered", [P, T, E])
        exps = sb("exps", [P, T, E])
        marks = sb("marks", [P, T, E])
        best = sb("best", [P, T])
        onehot = sb("onehot", [P, T, E], BF16)
        seen = sb("seen", [P, E], BF16)
        seen_add = sb("seen_add", [P, E])
        expsum = sb("expsum", [P, T])
        r_expsum = sb("r_expsum", [P, T])
        ranks = sb("ranks", [P, T, E])
        rank = sb("rank", [P, T])
        past = sb("past", [P, T])
        slot_f = sb("slot_f", [P, T])
        slot = sb("slot", [P, T], U32)
        w1_sb = [sb(f"w1_{i}", [P, KD, F]) for i in range(2)]
        w2_sb = [sb(f"w2_{i}", [P, KF, D]) for i in range(2)]
        q_rows = [sb(f"q_rows{i}", [SR, 2, ROW]) for i in range(2)]
        xdT = [sb(f"xdT{i}", [P, KD, CAP]) for i in range(2)]
        hidden = w_raw[:].rearrange("p w k d -> p (w k d)")[:, 0:KF * CAP].rearrange("p (k c) -> p k c", c=CAP)
        yT = sb("yT", [P, KD, CAP])
        weight = [sb(f"weight{i}", [SR, 2]) for i in range(2)]
        place = [sb(f"place{i}", [SR, 2], U32) for i in range(2)]
        resid = [sb(f"resid{i}", [SR, 2, D]) for i in range(2)]
        y_rows = [sb(f"y_rows{i}", [SR, 2, D]) for i in range(2)]

        bank = [es.enter_context(nc.psum_tensor(f"bank{i}", [P, 512], F32)) for i in range(8)]
        ps_scores, ps_probsT, ps_att, ps_misc = bank[0:2], bank[2:4], bank[4:6], bank[6:8]
        ps_hidden, ps_y, ps_xdT, ps_rows = bank[0:3], bank[3], bank[4], bank[5]

        pool_waited, dve_waited = sem("pool_waited"), sem("dve_waited")
        x_in = [sem(f"x_in{i}") for i in range(2)]
        ctx_in_s, w_in, small_in, mask_in = sem("ctx_in"), sem("w_in"), sem("small_in"), sem("mask_in")
        v_shifted, prefilled, x1_out = sem("v_shifted"), sem("prefilled"), sem("x1_out")
        scattered = sem("scattered")
        w1_in = [sem(f"w1_in{i}") for i in range(2)]
        w2_in = [sem(f"w2_in{i}") for i in range(2)]
        rows_in = [sem(f"rows_in{i}") for i in range(2)]
        y_out = [sem(f"y_out{i}") for i in range(2)]
        const_step, consts_ready, empty_ready = sem("const_step"), sem("consts_ready"), sem("empty_ready")
        mask_step, mask_ready, mask_set = sem("mask_step"), sem("mask_ready"), sem("mask_set")
        tanh_ready, bias_ready = sem("tanh_ready"), sem("bias_ready")
        pads_ready = sem("pads_ready")
        wT_ready, wT_taken = sem("wT_ready"), sem("wT_taken")
        x_stat, x_meanvar, x_eps, x_rstd = sem("x_stat"), sem("x_meanvar"), sem("x_eps"), sem("x_rstd")
        xn_ready, x_based = sem("xn_ready"), sem("x_based")
        xnT_ready, xnT_taken = sem("xnT_ready"), sem("xnT_taken")
        ctxT_ready, ctxT_taken = sem("ctxT_ready"), sem("ctxT_taken")
        q_ready, q_taken, q_split = sem("q_ready"), sem("q_taken"), sem("q_split")
        k_ready, k_taken = sem("k_ready"), sem("k_taken")
        v_ready, v_taken = sem("v_ready"), sem("v_taken")
        scores_ready, scores_taken = sem("scores_ready"), sem("scores_taken")
        exp_done, r_total_ready, probs_ready = sem("exp_done"), sem("r_total_ready"), sem("probs_ready")
        probsT_ready = sem("probsT_ready")
        probsT_taken = [sem("probsT_taken_dve"), sem("probsT_taken_act")]
        att_ready, att_even, att_taken = sem("att_ready"), sem("att_even"), sem("att_taken")
        o_ready, x1_ready = sem("o_ready"), sem("x1_ready")
        x1_stat, x1_meanvar, x1_eps, x1_rstd = sem("x1_stat"), sem("x1_meanvar"), sem("x1_eps"), sem("x1_rstd")
        x1n_ready = sem("x1n_ready")
        x1nT_ready, x1nT_taken = sem("x1nT_ready"), sem("x1nT_taken")
        logits_ready, logits_taken, exps_ready = sem("logits_ready"), sem("logits_taken"), sem("exps_ready")
        router_step, onehot_ready, weights_ready = sem("router_step"), sem("onehot_ready"), sem("weights_ready")
        counts_ready, counts_taken, slots_ready = sem("counts_ready"), sem("counts_taken"), sem("slots_ready")
        xdT_ready, xdT_taken, meta_taken = sem("xdT_ready"), sem("xdT_taken"), sem("meta_taken")
        hidden_ready, gelu_done = sem("hidden_ready"), sem("gelu_done")
        y_ready, yT_taken = sem("y_ready"), sem("yT_taken")
        yrows_ready, yrows_taken = sem("yrows_ready"), sem("yrows_taken")

        def value(n, per, k):
            return n * per + k

        def unit(i):
            half, g, wi = i // 8, i // 4 % 2, i % 4
            return half, g, wi, half * 4 + wi

        M_BANKS = [range(0, 3), range(3, 6), range(6, 8)]
        CTX_ORDER = (1, 0)
        RANK_STEPS = 5

        block = es.enter_context(nc.Block())

        @block.sync
        def _(sp):
            def load_ctx(n):
                if not isinstance(n, int) or n > 0:
                    sp.wait_ge(ctxT_ready, value(n - 1, 2, 2))
                sp.dma_start(ctx_rows[:], ctx_in[n].rearrange("(t p) d -> p t d", p=P)).then_inc(ctx_in_s, 16)

            def shift_v(n):
                sp.wait_ge(v_taken, value(n, 2, 2))
                if not isinstance(n, int) or n > 0:
                    sp.wait_ge(att_ready, value(n - 1, UNITS, UNITS))
                sp.dma_start(v_shift[WINDOW:P, :, :], v[0:WINDOW, :, :]).then_inc(v_shifted, 16)
                sp.dma_start(v_shift[0:WINDOW, 1:T, :], v[WINDOW:P, 0:T - 1, :]).then_inc(v_shifted, 16)

            def store_x1(n):
                sp.wait_ge(x1_ready, value(n, 2, 2))
                sp.dma_start(out[n].rearrange("(t p) d -> p t d", p=P), rows[:, :, D:2 * D]).then_inc(x1_out, 16)

            def load_w1(e, i):
                sp.dma_start(w1_sb[i][:], w1[e].rearrange("(k p) f -> p k f", p=P)).then_inc(w1_in[i], 16)

            def load_w2(e, i):
                sp.dma_start(w2_sb[i][:], w2[e].rearrange("(k p) d -> p k d", p=P)).then_inc(w2_in[i], 16)

            def load_rows(e, i):
                sp.dma_start(q_rows[i][:], queue[bass.ts(e, CAP), :].rearrange("(s p) c -> p s c", p=SR)
                             ).then_inc(rows_in[i], 16)

            sp.dma_start(x_all[:, 0], x[0].rearrange("(t p) d -> p t d", p=P)).then_inc(x_in[0], 16)
            load_ctx(0)
            for i, w in enumerate((W_q, W_k, W_v, W_o)):
                sp.dma_start(w_raw[:, i], w.rearrange("(t p) d -> p t d", p=P)).then_inc(w_in, 16)
            sp.dma_start(gate_raw[:], gate_w).then_inc(w_in, 16)
            for i, b in enumerate((b_q, b_k)):
                sp.dma_start(bias_qk_raw[:, i], b.rearrange("(g p) -> p g", p=P),
                             allow_slow_non_contiguous=True).then_inc(small_in, 16)
            sp.dma_start(bias_v[:], b_v.partition_broadcast(P)).then_inc(small_in, 16)
            sp.dma_start(bias_o[:], b_o.partition_broadcast(P)).then_inc(small_in, 16)
            sp.dma_start(gates[:, 0:1], g_xattn.partition_broadcast(P)).then_inc(small_in, 16)
            sp.dma_start(gates[:, 1:2], g_ffn.partition_broadcast(P)).then_inc(small_in, 16)
            sp.dma_start(mask_u8[:], mask.partition_broadcast(P)).then_inc(mask_in, 16)
            for n in range(1, B):
                sp.dma_start(x_all[:, n], x[n].rearrange("(t p) d -> p t d", p=P)).then_inc(x_in[1], 16)
            sp.wait_ge(empty_ready, 2)
            sp.dma_start(queue.rearrange("(s p) c -> p s c", p=P),
                         empty_row[:].unsqueeze(1).to_broadcast([P, E * CAP // P, ROW])).then_inc(prefilled, 16)
            for e in range(2):
                load_w1(e, e)
                load_w2(e, e)
            shift_v(0)
            load_ctx(1)
            shift_v(1)
            with sp.Fori(1, B - 1) as b:
                store_x1(b - 1)
                load_ctx(b + 1)
                shift_v(b + 1)
            store_x1(B - 2)
            store_x1(B - 1)

            sp.wait_ge(scattered, 16 * T * B)
            for e in range(2):
                load_rows(e, e)

            def reload(e, i):
                sp.wait_ge(xdT_ready, e + 1)
                sp.wait_ge(meta_taken, e + 1)
                load_rows(e + 2, i)
                sp.wait_ge(hidden_ready, 3 * e + 3)
                load_w1(e + 2, i)
                sp.wait_ge(y_ready, e + 1)
                load_w2(e + 2, i)

            with sp.Fori(0, E // 2 - 1) as turn:
                reload(2 * turn, 0)
                reload(2 * turn + 1, 1)

        @block.gpsimd
        def _(pool):
            c = 0
            pool.memset(ident[:], 0.0)
            pool.memset(causal[:], 1.0)
            pool.memset(before[:], 1.0)
            pool.memset(head_mask[:], 1.0)
            pool.memset(parity_mask[:], 0.0)
            pool.memset(ones[:], 1.0)
            pool.memset(minus_half[:], -0.5)
            pool.memset(eps[:], EPS)
            pool.memset(seen[:], 0.0)
            pool.memset(empty_row[:, 0:ROW - 1], 0.0).then_inc(empty_ready, 1)
            pool.memset(empty_row[:, ROW - 1:ROW], NO_TOKEN).then_inc(empty_ready, 1)
            pool.memset(kT[:, :, 0:WINDOW], 0.0).then_inc(pads_ready, 1)
            pool.memset(v_shift[0:WINDOW, 0:1, :], 0.0).then_inc(pads_ready, 1)
            pool.memset(key_valid[:, :, 0:WINDOW], 0.0).then_inc(const_step, 1)
            pool.wait_ge(const_step, 1)
            pool.affine_select(out=ident[:], in_=ident[:], compare_op=ALU.not_equal, fill=1.0, base=0,
                               pattern=[[-1, P]], channel_multiplier=1)
            pool.affine_select(out=before[:], in_=before[:], compare_op=ALU.is_ge, fill=0.0, base=-1,
                               pattern=[[1, P]], channel_multiplier=-1).then_inc(const_step, 1)
            for h in range(2):
                q = slice(h * WINDOW, (h + 1) * WINDOW)
                pool.wait_ge(const_step, 2 + h)
                pool.affine_select(out=causal[q, WINDOW:], in_=causal[q, WINDOW:], compare_op=ALU.is_ge, fill=0.0,
                                   base=0, pattern=[[-1, WINDOW]], channel_multiplier=1).then_inc(const_step, 1)
            pool.wait_ge(const_step, 4)
            pool.affine_select(out=head_mask[:], in_=head_mask[:], compare_op=ALU.is_ge, fill=0.0, base=0,
                               pattern=[[-HD, HG]], channel_multiplier=1).then_inc(const_step, 1)
            pool.wait_ge(const_step, 5)
            pool.affine_select(out=head_mask[:], in_=head_mask[:], compare_op=ALU.is_ge, fill=0.0, base=HD - 1,
                               pattern=[[HD, HG]], channel_multiplier=-1).then_inc(const_step, 1)
            pool.iota(countdown[:], pattern=[[0, T], [-1, E]], base=E, channel_multiplier=0,
                      allow_small_or_imprecise_dtypes=True)
            pool.iota(token_no[:], pattern=[[P, B * T]], base=0, channel_multiplier=1,
                      allow_small_or_imprecise_dtypes=True).then_inc(consts_ready, 1)
            pool.wait_ge(const_step, 6)
            for h in range(HG):
                pool.tensor_tensor(parity_mask[:, h % 2:h % 2 + 1], parity_mask[:, h % 2:h % 2 + 1],
                                   head_mask[:, h:h + 1], ALU.add).then_inc(const_step, 1)
                pool.wait_ge(const_step, 7 + h)

            def x_rstd_of(n):
                pool.wait_ge(x_meanvar, value(n, 1, 1))
                pool.tensor_tensor(var_eps[:], mean_var[:, :, 1], eps[:], ALU.add).then_inc(x_eps, 1)
                pool.wait_ge(x_eps, value(n, 1, 1))
                pool.tensor_tensor(rstd[:], var_eps[:], minus_half[:], ALU.pow).then_inc(x_rstd, 1)

            def base_of(n):
                pool.wait_ge(xn_ready, value(n, 1, 1))
                pool.wait_ge(bias_ready, 2)
                pool.tensor_tensor(x_all[:, n], x_all[:, n], bias_og[:].unsqueeze(1).to_broadcast([P, T, D]),
                                   ALU.add).then_inc(x_based, 1)

            def norm(n, i):
                pool.wait_ge(r_total_ready, value(n, UNITS, i + 1))
                pool.tensor_tensor(probs[:, i % NP_], probs[:, i % NP_],
                                   r_total[:, i % NP_].unsqueeze(2).to_broadcast([P, PAIRS, 2 * WINDOW]),
                                   ALU.mult).then_inc(probs_ready, 1)

            def x1_rstd_of(n):
                pool.wait_ge(x1_meanvar, value(n, 1, 1))
                pool.tensor_tensor(var_eps2[:], mean_var2[:, :, 1], eps[:], ALU.add).then_inc(x1_eps, 1)
                pool.wait_ge(x1_eps, value(n, 1, 1))
                pool.tensor_tensor(rstd2[:], var_eps2[:], minus_half[:], ALU.pow).then_inc(x1_rstd, 1)

            def scatter(n):
                pool.wait_ge(prefilled, 16)
                pool.wait_ge(slots_ready, value(n, 1, 1))
                pool.wait_ge(weights_ready, value(n, 2, 2))
                pool.wait_ge(x1n_ready, value(n, 1, 1))
                pool.sem_inc(pool_waited, 1)
                for t in range(T):
                    pool.indirect_dma_start(out=queue, out_offset=bass.IndirectOffsetOnAxis(ap=slot[:, t:t + 1], axis=0),
                                            in_=rows[:, t, :], in_offset=None, bounds_check=E * CAP - 1,
                                            oob_is_err=False).then_inc(scattered, 16)

            def body(b, post, prep):
                for i in range(UNITS + 1):
                    if i == 0 and prep:
                        x_rstd_of(b + 1)
                    if 1 <= i <= UNITS:
                        norm(b, i - 1)
                    if i == 3 and prep:
                        base_of(b + 1)
                    if i == 4 and post:
                        x1_rstd_of(b - 1)
                    if i == UNITS and post:
                        scatter(b - 1)

            x_rstd_of(0)
            base_of(0)
            body(0, False, True)
            with pool.Fori(1, B - 1) as b:
                body(b, True, True)
            body(B - 1, True, False)
            x1_rstd_of(B - 1)
            scatter(B - 1)

            def place_rows(e, i):
                pool.wait_ge(x1_out, 16 * B)
                pool.wait_ge(yrows_taken, e + 1)
                pool.sem_inc(pool_waited, 1)
                for s in range(2):
                    pool.indirect_dma_start(out=out_rows,
                                            out_offset=bass.IndirectOffsetOnAxis(ap=place[i][:, s:s + 1], axis=0),
                                            in_=y_rows[i][:, s, :], in_offset=None, bounds_check=B * S - 1,
                                            oob_is_err=False).then_inc(y_out[i], 16)

            with pool.Fori(0, E // 2) as turn:
                place_rows(2 * turn, 0)
                place_rows(2 * turn + 1, 1)
            for i in range(2):
                pool.wait_ge(y_out[i], 16 * E)

        @block.scalar
        def _(act):
            act.wait_ge(small_in, 6 * 16)
            act.activation(tanh_g[:], gates[:], ACT.Tanh).then_inc(tanh_ready, 1)

            def take_wT(i):
                act.wait_ge(wT_ready, i + 1)
                act.activation(wT[:, i], bank[i][:].rearrange("p (k d) -> p k d", k=KD), ACT.Copy).then_inc(wT_taken, 1)

            def take_xnT(n, k):
                act.wait_ge(xnT_ready, value(n, 2, k + 1))
                act.activation(xnT[:, k], ps_misc[k][:], ACT.Copy).then_inc(xnT_taken, 1)

            def take_q(n, g):
                act.wait_ge(q_ready, value(n, 2, g + 1))
                if not isinstance(n, int) or n > 0:
                    act.wait_ge(q_split, value(n - 1, 2 * CHUNKS, 2 * CHUNKS))
                act.activation(qT[:, g], ps_misc[g][:], ACT.Identity, bias=bias_q[:, g:g + 1],
                               scale=-float(HD) ** -0.5).then_inc(q_taken, 1)

            def take_k(n, g):
                act.wait_ge(k_ready, value(n, 2, g + 1))
                if not isinstance(n, int) or n > 0:
                    act.wait_ge(scores_ready, value(n - 1, UNITS, UNITS))
                act.activation(kT[:, g, WINDOW:], ps_misc[g][:], ACT.Identity,
                               bias=bias_qk_raw[:, 1, g:g + 1]).then_inc(k_taken, 1)

            def exp(n, i):
                act.wait_ge(scores_taken, value(n, UNITS, i + 1))
                for j in range(PAIRS):
                    last = act.activation(probs[:, i % NP_, j], probs[:, i % NP_, j], ACT.Exp, scale=-1.0,
                                          bias=low[:, i % NP_, j:j + 1], accum_out=total[:, i % NP_, j:j + 1])
                last.then_inc(exp_done, 1)

            def take_probsT(n, i):
                act.wait_ge(probsT_ready, value(n, UNITS, i + 1))
                if i >= 2:
                    act.wait_ge(att_ready, value(n, UNITS, i - 1))
                elif not isinstance(n, int) or n > 0:
                    act.wait_ge(att_ready, value(n - 1, UNITS, UNITS + i - 1))
                act.activation(probsT[:, i % 2], ps_probsT[i % 2][:].rearrange("p (j q) -> p j q", j=PAIRS),
                               ACT.Copy).then_inc(probsT_taken[1], 1)

            def take_x1nT(n, k):
                act.wait_ge(x1nT_ready, value(n, 2, k + 1))
                act.activation(x1nT[:, k], ps_misc[k][:], ACT.Copy).then_inc(x1nT_taken, 1)

            def exp_logits(n):
                act.wait_ge(logits_taken, value(n, 1, 1))
                act.activation(exps[:], lowered[:], ACT.Exp).then_inc(exps_ready, 1)

            def body(b, post, prep):
                for i in range(UNITS + 4):
                    if i < UNITS:
                        exp(b, i)
                    if 3 <= i < UNITS + 3 and i % 2 == 0:
                        take_probsT(b, i - 3)
                    if prep and i in (4, 5):
                        take_xnT(b + 1, i - 4)
                    if prep and i in (7, 8):
                        take_q(b + 1, i - 7)
                    if post and i in (10, 11):
                        take_x1nT(b - 1, i - 10)
                    if post and i == 14:
                        exp_logits(b - 1)
                    if prep and i in (17, 18):
                        take_k(b + 1, i - 17)

            for i in range(4):
                take_wT(i)
            for k in range(KD):
                take_xnT(0, k)
            act.wait_ge(bias_ready, 1)
            for g in range(KD):
                take_q(0, g)
            for g in range(KD):
                take_k(0, g)
            body(0, False, True)
            with act.Fori(1, B - 1) as b:
                body(b, True, True)
            body(B - 1, True, False)
            for k in range(KD):
                take_x1nT(B - 1, k)
            exp_logits(B - 1)

            def gelu(e, first):
                for m, ms in enumerate(M_BANKS):
                    act.wait_ge(hidden_ready, 3 * e + m + 1)
                    if not first:
                        act.wait_ge(y_ready, e)
                    n = len(ms) * CAP
                    act.activation(hidden[:, ms[0]:ms[-1] + 1, :], ps_hidden[m][:, 0:n].rearrange("p (m c) -> p m c", c=CAP),
                                   ACT.Gelu_apprx_tanh).then_inc(gelu_done, 1)

            gelu(0, True)
            gelu(1, False)
            with act.Fori(1, E // 2) as turn:
                gelu(2 * turn, False)
                gelu(2 * turn + 1, False)

        @block.vector
        def _(dve):
            dve.wait_ge(small_in, 6 * 16)
            dve.tensor_scalar(bias_q[:], bias_qk_raw[:, 0], -float(HD) ** -0.5, None, ALU.mult).then_inc(bias_ready, 1)
            dve.wait_ge(tanh_ready, 1)
            dve.tensor_scalar(bias_og[:], bias_o[:], tanh_g[:, 0:1], None, ALU.mult).then_inc(bias_ready, 1)

            def x_stats(n):
                if isinstance(n, int) and n == 0:
                    dve.wait_ge(x_in[0], 16)
                else:
                    dve.wait_ge(x_in[1], 16 * (B - 1))
                    dve.wait_ge(xn_ready, value(n - 1, 1, 1))
                for t in range(T):
                    last = dve.bn_stats(stats[:, t], x_all[:, n, t])
                last.then_inc(x_stat, 1)
                dve.wait_ge(x_stat, value(n, 1, 1))
                dve.sem_inc(dve_waited, 1)
                for t in range(T):
                    last = dve.bn_aggr(mean_var[:, t], stats[:, t])
                last.then_inc(x_meanvar, 1)

            def x_norm(n):
                dve.wait_ge(x_rstd, value(n, 1, 1))
                if not isinstance(n, int) or n > 0:
                    dve.wait_ge(xnT_ready, value(n - 1, 2, 2))
                for t in range(T):
                    last = dve.tensor_scalar(xn[:, t], x_all[:, n, t], mean_var[:, t, 0:1], rstd[:, t:t + 1],
                                             ALU.subtract, ALU.mult)
                last.then_inc(xn_ready, 1)

            def take_ctxT(n, j):
                k = CTX_ORDER[j]
                dve.wait_ge(ctxT_ready, value(n, 2, j + 1))
                dve.tensor_copy(ctxT[:, k], ps_misc[k][:]).then_inc(ctxT_taken, 1)

            def take_v(n, k):
                dve.wait_ge(v_ready, value(n, 2, k + 1))
                if not isinstance(n, int) or n > 0:
                    dve.wait_ge(att_ready, value(n - 1, UNITS, UNITS))
                    dve.wait_ge(v_shifted, 32 * n)
                dve.tensor_tensor(v[:, 2 * k:2 * k + 2], ps_misc[k][:].rearrange("p (t d) -> p t d", d=D),
                                  bias_v[:].unsqueeze(1).to_broadcast([P, 2, D]), ALU.add).then_inc(v_taken, 1)

            def low_of(n, i):
                _, _, _, w = unit(i)
                dve.wait_ge(scores_ready, value(n, UNITS, i + 1))
                if i >= NP_:
                    dve.wait_ge(probsT_ready, value(n, UNITS, i - NP_ + 1))
                elif not isinstance(n, int) or n > 0:
                    dve.wait_ge(probsT_ready, value(n - 1, UNITS, UNITS + i - NP_ + 1))
                if i == 0:
                    if isinstance(n, int) and n == 0:
                        dve.wait_ge(mask_ready, 1)
                    else:
                        dve.wait_ge(scores_taken, value(n - 1, UNITS, UNITS))
                    dve.tensor_copy(mask_now[:], mask_add[:, n]).then_inc(mask_set, 1)
                    dve.wait_ge(mask_set, value(n, 1, 1))
                dve.sem_inc(dve_waited, 1)
                for j in range(PAIRS):
                    last = dve.tensor_tensor_reduce(
                        probs[:, i % NP_, j], ps_scores[i % 2][:, j * P:(j + 1) * P], mask_now[:, w % 2, w // 2],
                        1.0, 3.0e38, ALU.add, ALU.min, low[:, i % NP_, j:j + 1])
                last.then_inc(scores_taken, 1)

            def r_total_of(n, i):
                dve.wait_ge(exp_done, value(n, UNITS, i + 1))
                dve.reciprocal(r_total[:, i % NP_], total[:, i % NP_]).then_inc(r_total_ready, 1)

            def take_probsT(n, i):
                dve.wait_ge(probsT_ready, value(n, UNITS, i + 1))
                if i >= 2:
                    dve.wait_ge(att_ready, value(n, UNITS, i - 1))
                elif not isinstance(n, int) or n > 0:
                    dve.wait_ge(att_ready, value(n - 1, UNITS, UNITS + i - 1))
                dve.tensor_copy(probsT[:, i % 2], ps_probsT[i % 2][:].rearrange("p (j q) -> p j q", j=PAIRS)
                                ).then_inc(probsT_taken[0], 1)

            def take_att(n, c):
                half, g, _, _ = unit(4 * c)
                dve.wait_ge(att_ready, value(n, UNITS, 4 * c + 4))
                if not isinstance(n, int) or n > 0:
                    dve.wait_ge(o_ready, value(n - 1, 2, 2))
                src = ps_att[c % 2][:].rearrange("p (w e q) -> p w e q", w=4, e=2)
                dst = attT[:, g, half * 4 * WINDOW:(half + 1) * 4 * WINDOW].rearrange("p (w q) -> p w q", q=WINDOW)
                dve.tensor_scalar(dst, src[:, :, 0], parity_mask[:, 0:1], None, ALU.mult).then_inc(att_even, 1)
                dve.wait_ge(att_even, value(n, CHUNKS, c + 1))
                dve.scalar_tensor_tensor(dst, src[:, :, 1], parity_mask[:, 1:2], dst, ALU.mult, ALU.add
                                         ).then_inc(att_taken, 1)

            def split_q(n, part):
                c, h0 = part // 2, part % 2 * 4
                half, g, _, _ = unit(4 * c)
                if part % 2 == 0:
                    dve.wait_ge(q_taken, value(n, 2, g + 1))
                    if not isinstance(n, int) or n > 0:
                        dve.wait_ge(scores_ready, value(n - 1, UNITS, 4 * c + 4))
                src = qT[:, g, half * 4 * WINDOW:(half + 1) * 4 * WINDOW].rearrange("p (w q) -> p w q", q=WINDOW)
                for h in range(h0, h0 + 4):
                    last = dve.tensor_scalar(q_heads[:, g, half * 4:half * 4 + 4, h, :], src,
                                              head_mask[:, h:h + 1], None, ALU.mult)
                last.then_inc(q_split, 1)

            def x1_of(n, k):
                dve.wait_ge(o_ready, value(n, 2, k + 1))
                dve.wait_ge(x_based, value(n, 1, 1))
                if not isinstance(n, int) or n > 0:
                    dve.wait_ge(x1_out, 16 * n)
                    dve.wait_ge(scattered, 16 * T * n)
                dve.scalar_tensor_tensor(rows[:, 2 * k:2 * k + 2, D:2 * D],
                                         ps_misc[k][:].rearrange("p (t d) -> p t d", d=D), tanh_g[:, 0:1],
                                         x_all[:, n, 2 * k:2 * k + 2], ALU.mult, ALU.add).then_inc(x1_ready, 1)

            def x1_stats(n):
                dve.wait_ge(x1_ready, value(n, 2, 2))
                for t in range(T):
                    last = dve.bn_stats(stats2[:, t], rows[:, t, D:2 * D])
                last.then_inc(x1_stat, 1)
                dve.wait_ge(x1_stat, value(n, 1, 1))
                dve.sem_inc(dve_waited, 1)
                for t in range(T):
                    last = dve.bn_aggr(mean_var2[:, t], stats2[:, t])
                last.then_inc(x1_meanvar, 1)

            def x1_norm(n):
                dve.wait_ge(x1_rstd, value(n, 1, 1))
                for t in range(T):
                    last = dve.tensor_scalar(rows[:, t, 0:D], rows[:, t, D:2 * D], mean_var2[:, t, 0:1],
                                             rstd2[:, t:t + 1], ALU.subtract, ALU.mult)
                last.then_inc(x1n_ready, 1)

            def choose(n):
                def done(k):
                    dve.wait_ge(router_step, value(n, RANK_STEPS + 3, k))
                dve.wait_ge(logits_ready, value(n, 1, 1))
                logits = ps_misc[0][:, 0:T * E].rearrange("p (t e) -> p t e", e=E)
                dve.tensor_reduce(top[:], logits, AX.X, ALU.max).then_inc(router_step, 1)
                done(1)
                dve.tensor_tensor(lowered[:], logits, top[:].unsqueeze(2).to_broadcast([P, T, E]), ALU.subtract
                                  ).then_inc(logits_taken, 1)
                dve.wait_ge(logits_taken, value(n, 1, 1))
                dve.scalar_tensor_tensor(marks[:], lowered[:], 0.0, countdown[:], ALU.is_ge, ALU.mult
                                         ).then_inc(router_step, 1)
                done(2)
                dve.tensor_reduce(best[:], marks[:], AX.X, ALU.max).then_inc(router_step, 1)
                done(3)
                dve.tensor_tensor(onehot[:], marks[:], best[:].unsqueeze(2).to_broadcast([P, T, E]), ALU.is_equal
                                  ).then_inc(onehot_ready, 1)

            def rank_of(n):
                def done(k):
                    dve.wait_ge(router_step, value(n, RANK_STEPS + 3, 3 + k))
                dve.wait_ge(exps_ready, value(n, 1, 1))
                dve.tensor_reduce(expsum[:], exps[:], AX.X, ALU.add).then_inc(router_step, 1)
                done(1)
                dve.reciprocal(r_expsum[:], expsum[:]).then_inc(router_step, 1)
                done(2)
                dve.tensor_scalar(rows[:, :, 2 * D], r_expsum[:], tanh_g[:, 1:2], None, ALU.mult
                                  ).then_inc(weights_ready, 1)
                dve.tensor_copy(rows[:, :, 2 * D + 1], token_no[:, bass.ts(n, T)]).then_inc(weights_ready, 1)
                dve.wait_ge(counts_ready, value(n, 1, 1))
                counts = ps_misc[1][:, 0:T * E].rearrange("p (t e) -> p t e", e=E)
                dve.tensor_tensor(ranks[:], counts, onehot[:], ALU.mult).then_inc(counts_taken, 1)
                dve.wait_ge(counts_taken, value(n, 1, 1))
                dve.tensor_reduce(rank[:], ranks[:], AX.X, ALU.add).then_inc(router_step, 1)
                dve.tensor_reduce(seen_add[:], onehot[:].rearrange("p t e -> p e t"), AX.X, ALU.add
                                  ).then_inc(router_step, 1)
                done(4)
                dve.tensor_tensor(seen[:], seen[:], seen_add[:], ALU.add)
                dve.tensor_scalar(past[:], rank[:], float(CAP), DROPPED, ALU.is_ge, ALU.mult)
                dve.scalar_tensor_tensor(slot_f[:], best[:], -float(CAP), rank[:], ALU.mult, ALU.add
                                         ).then_inc(router_step, 1)
                done(5)
                dve.scalar_tensor_tensor(slot[:], slot_f[:], float(E * CAP), past[:], ALU.add, ALU.add
                                         ).then_inc(slots_ready, 1)

            def body(b, post, prep):
                for i in range(UNITS + 5):
                    if i < UNITS:
                        low_of(b, i)
                    if 1 <= i <= UNITS:
                        r_total_of(b, i - 1)
                    if 3 <= i < UNITS + 3 and i % 2 == 1:
                        take_probsT(b, i - 3)
                    if i in (8, 12, 16, 20):
                        take_att(b, (i - 8) // 4)
                    if prep and i == 0:
                        x_stats(b + 1)
                    if prep and i == 2:
                        x_norm(b + 1)
                    if post and i in (1, 2):
                        x1_of(b - 1, i - 1)
                    if post and i == 3:
                        x1_stats(b - 1)
                    if post and i == 5:
                        x1_norm(b - 1)
                    if prep and i in (9, 10, 11, 12, 14, 15, 17, 18):
                        split_q(b + 1, (9, 10, 11, 12, 14, 15, 17, 18).index(i))
                    if post and i == 13:
                        choose(b - 1)
                    if prep and i in (14, 15):
                        take_ctxT(b + 1, i - 14)
                    if post and i == 16:
                        rank_of(b - 1)
                    if prep and i in (19, 20):
                        take_v(b + 1, i - 19)

            def take_gateT():
                dve.wait_ge(wT_ready, 5)
                dve.tensor_copy(gateT[:], bank[4][:, 0:KD * E].rearrange("p (k e) -> p k e", e=E)).then_inc(wT_taken, 1)

            x_stats(0)
            x_norm(0)
            take_gateT()
            for k in range(KD):
                take_ctxT(0, k)
            dve.wait_ge(mask_in, 16)
            dve.wait_ge(consts_ready, 1)
            dve.tensor_copy(key_valid[:, :, WINDOW:], mask_u8[:]).then_inc(mask_step, 1)
            dve.wait_ge(mask_step, 1)
            for n in range(B):
                for e in range(2):
                    keys = key_valid[:, n, e * WINDOW:e * WINDOW + S].rearrange("p (w k) -> p w k", k=2 * WINDOW)
                    dve.tensor_tensor(mask_add[:, n, e], keys,
                                       causal[:].unsqueeze(1).to_broadcast([P, NW // 2, 2 * WINDOW]),
                                       ALU.mult).then_inc(mask_step, 1)
            dve.wait_ge(mask_step, 1 + 2 * B)
            dve.tensor_scalar(mask_add[:], mask_add[:], -MASKED, MASKED, ALU.mult, ALU.add).then_inc(mask_ready, 1)

            for part in range(2 * CHUNKS):
                split_q(0, part)
            for k in range(KD):
                take_v(0, k)
            body(0, False, True)
            with dve.Fori(1, B - 1) as b:
                body(b, True, True)
            body(B - 1, True, False)
            for k in range(2):
                x1_of(B - 1, k)
            x1_stats(B - 1)
            x1_norm(B - 1)
            choose(B - 1)
            rank_of(B - 1)

            def take_xd(e, i, first):
                dve.wait_ge(xdT_ready, e + 1)
                if not first:
                    dve.wait_ge(hidden_ready, 3 * e - 3)
                    dve.wait_ge(y_out[i], 16 * (e - i))
                dve.tensor_copy(xdT[i][:], ps_xdT[:, 0:KD * CAP].rearrange("p (k c) -> p k c", c=CAP)
                                ).then_inc(xdT_taken, 1)
                dve.tensor_copy(place[i][:], q_rows[i][:, :, 2 * D + 1])
                dve.tensor_copy(weight[i][:], q_rows[i][:, :, 2 * D])
                dve.tensor_copy(resid[i][:], q_rows[i][:, :, D:2 * D]).then_inc(meta_taken, 1)

            def take_yT(e):
                dve.wait_ge(y_ready, e + 1)
                dve.tensor_copy(yT[:], ps_y[:, 0:KD * CAP].rearrange("p (k c) -> p k c", c=CAP)).then_inc(yT_taken, 1)

            def take_yrows(e, i):
                dve.wait_ge(yrows_ready, e + 1)
                dve.wait_ge(meta_taken, e + 1)
                for s in range(2):
                    last = dve.scalar_tensor_tensor(y_rows[i][:, s], ps_rows[0:SR, s * D:(s + 1) * D],
                                                    weight[i][:, s:s + 1], resid[i][:, s], ALU.mult, ALU.add)
                last.then_inc(yrows_taken, 1)

            def expert(e, i, before_it, after_it, first):
                if before_it:
                    take_yrows(e - 1, 1 - i)
                if after_it:
                    take_xd(e + 1, 1 - i, first)
                take_yT(e)

            take_xd(0, 0, True)
            expert(0, 0, False, True, True)
            expert(1, 1, True, True, False)
            with dve.Fori(1, E // 2 - 1) as turn:
                expert(2 * turn, 0, True, True, False)
                expert(2 * turn + 1, 1, True, True, False)
            expert(E - 2, 0, True, True, False)
            expert(E - 1, 1, True, False, False)
            take_yrows(E - 1, 1)

        @block.tensor
        def _(pe):
            pe.wait_ge(consts_ready, 1)
            pe.wait_ge(w_in, 5 * 16)
            for i in range(4):
                for k in range(KD):
                    for d in range(KD):
                        last = pe.transpose(bank[i][:, k * D + d * P:k * D + (d + 1) * P],
                                            w_raw[:, i, d, k * P:(k + 1) * P], ident[:])
                last.then_inc(wT_ready, 1)
            for k in range(KD):
                last = pe.transpose(bank[4][:, k * E:(k + 1) * E], gate_raw[:, k * P:(k + 1) * P], ident[0:E, 0:E])
            last.then_inc(wT_ready, 1)
            pe.wait_ge(wT_taken, 5)

            def xnT_of(n, k, free, least):
                pe.wait_ge(xn_ready, value(n, 1, 1))
                if free is not None:
                    pe.wait_ge(free, least)
                for t in range(T):
                    last = pe.transpose(ps_misc[k][:, t * P:(t + 1) * P], xn[:, t, k * P:(k + 1) * P], ident[:])
                last.then_inc(xnT_ready, 1)

            def ctxT_of(n, j, free, least):
                k = CTX_ORDER[j]
                pe.wait_ge(ctx_in_s, 16 * (n + 1))
                pe.wait_ge(free, least)
                for t in range(T):
                    last = pe.transpose(ps_misc[k][:, t * P:(t + 1) * P], ctx_rows[:, t, k * P:(k + 1) * P], ident[:])
                last.then_inc(ctxT_ready, 1)

            def q_of(n, g):
                pe.wait_ge(xnT_taken, value(n, 2, 2))
                for k in range(KD):
                    last = pe.matmul(ps_misc[g][:], wT[:, 0, k, g * P:(g + 1) * P], xnT[:, k], start=(k == 0),
                                     stop=(k == KD - 1))
                last.then_inc(q_ready, 1)

            def k_of(n, g, free, least):
                pe.wait_ge(free, least)
                pe.wait_ge(ctxT_taken, value(n, 2, 2))
                for k in range(KD):
                    last = pe.matmul(ps_misc[g][:], wT[:, 1, k, g * P:(g + 1) * P], ctxT[:, k], start=(k == 0),
                                     stop=(k == KD - 1))
                last.then_inc(k_ready, 1)

            def v_of(n, m):
                pe.wait_ge(k_taken, value(n, 2, m + 1))
                for t in range(2 * m, 2 * m + 2):
                    for k in range(KD):
                        last = pe.matmul(ps_misc[m][:, t % 2 * D:(t % 2 + 1) * D], ctxT[:, k, t * P:(t + 1) * P],
                                         wT[:, 2, k], start=(k == 0), stop=(k == KD - 1))
                last.then_inc(v_ready, 1)

            def scores(n, i):
                _, g, _, w = unit(i)
                if i % 4 == 0:
                    pe.wait_ge(q_split, value(n, 2 * CHUNKS, 2 * (i // 4) + 2))
                if i == 0:
                    pe.wait_ge(k_taken, value(n, 2, 2))
                if i >= 2:
                    pe.wait_ge(scores_taken, value(n, UNITS, i - 1))
                elif not isinstance(n, int) or n > 0:
                    pe.wait_ge(scores_taken, value(n - 1, UNITS, UNITS + i - 1))
                for j in range(PAIRS):
                    last = pe.matmul(ps_scores[i % 2][:, j * P:(j + 1) * P],
                                     q_heads[:, g, w, 2 * j:2 * j + 2, :],
                                     kT[:, g, w * WINDOW:w * WINDOW + 2 * WINDOW], start=True, stop=True)
                last.then_inc(scores_ready, 1)

            def probsT_of(n, i):
                pe.wait_ge(probs_ready, value(n, UNITS, i + 1))
                if i >= 2:
                    pe.wait_ge(probsT_taken[i % 2], value(n, UNITS // 2, i // 2))
                elif not isinstance(n, int) or n > 0:
                    pe.wait_ge(probsT_taken[i % 2], value(n - 1, UNITS // 2, UNITS // 2))
                for j in range(PAIRS):
                    last = pe.transpose(ps_probsT[i % 2][:, j * P:(j + 1) * P], probs[:, i % NP_, j], ident[:])
                last.then_inc(probsT_ready, 1)

            def attend(n, i):
                _, g, wi, w = unit(i)
                c = i // 4
                pe.wait_ge(probsT_taken[i % 2], value(n, UNITS // 2, i // 2 + 1))
                if i == 0:
                    pe.wait_ge(v_taken, value(n, 2, 2))
                    pe.wait_ge(v_shifted, 32 * (n + 1))
                if wi == 0:
                    if c >= 2:
                        pe.wait_ge(att_taken, value(n, CHUNKS, c - 1))
                    elif not isinstance(n, int) or n > 0:
                        pe.wait_ge(att_taken, value(n - 1, CHUNKS, CHUNKS + c - 1))
                src = v if w % 2 else v_shift
                for j in range(PAIRS):
                    last = pe.matmul(ps_att[c % 2][j * 32:(j + 1) * 32, wi * P:(wi + 1) * P],
                                     src[:, w // 2, g * P + j * 32:g * P + (j + 1) * 32], probsT[:, i % 2, j],
                                     start=True, stop=True)
                last.then_inc(att_ready, 1)

            def project(n, m, free, least):
                pe.wait_ge(free, least)
                pe.wait_ge(att_taken, value(n, CHUNKS, CHUNKS))
                for t in range(2 * m, 2 * m + 2):
                    for g in range(KD):
                        last = pe.matmul(ps_misc[m][:, t % 2 * D:(t % 2 + 1) * D], attT[:, g, t * P:(t + 1) * P],
                                         wT[:, 3, g], start=(g == 0), stop=(g == KD - 1))
                last.then_inc(o_ready, 1)

            def x1nT_of(n, k, free, least):
                pe.wait_ge(x1n_ready, value(n, 1, 1))
                pe.wait_ge(free, least)
                for t in range(T):
                    last = pe.transpose(ps_misc[k][:, t * P:(t + 1) * P], rows[:, t, k * P:(k + 1) * P], ident[:])
                last.then_inc(x1nT_ready, 1)

            def route(n):
                pe.wait_ge(x1nT_taken, value(n, 2, 2))
                for t in range(T):
                    for k in range(KD):
                        last = pe.matmul(ps_misc[0][:, t * E:(t + 1) * E], x1nT[:, k, t * P:(t + 1) * P],
                                         gateT[:, k], start=(k == 0), stop=(k == KD - 1))
                last.then_inc(logits_ready, 1)

            def count(n, free, least):
                pe.wait_ge(free, least)
                pe.wait_ge(onehot_ready, value(n, 1, 1))
                if not isinstance(n, int) or n > 0:
                    pe.wait_ge(slots_ready, value(n - 1, 1, 1))
                bank_ = ps_misc[1][:, 0:T * E]
                pe.matmul(bank_, ones[:], seen[:].unsqueeze(1).to_broadcast([P, T, E]), start=True, stop=False,
                          skip_group_check=True)
                for t in range(T - 1):
                    pe.matmul(bank_[:, (t + 1) * E:], ones[:],
                              onehot[:, t:t + 1].to_broadcast([P, T - 1 - t, E]), start=False, stop=False,
                              skip_group_check=True)
                pe.matmul(bank_, before[:], onehot[:], start=False, stop=True, skip_group_check=True
                          ).then_inc(counts_ready, 1)

            def body(b, post, prep):
                for i in range(UNITS + 4):
                    if i < UNITS:
                        scores(b, i)
                    if post and i in (0, 1):
                        project(b - 1, i, v_taken, value(b, 2, i + 1))
                    if prep and i in (3, 4):
                        if post:
                            xnT_of(b + 1, i - 3, x1_ready, value(b - 1, 2, i - 2))
                        else:
                            xnT_of(b + 1, i - 3, v_taken, value(b, 2, i - 2))
                    if prep and i in (6, 7):
                        q_of(b + 1, i - 6)
                    if post and i in (9, 10):
                        if prep:
                            x1nT_of(b - 1, i - 9, q_taken, value(b + 1, 2, i - 8))
                        else:
                            x1nT_of(b - 1, i - 9, x1_ready, value(b - 1, 2, i - 8))
                    if post and i == 12:
                        route(b - 1)
                    if prep and i == 13:
                        if post:
                            ctxT_of(b + 1, 0, x1nT_taken, value(b - 1, 2, 2))
                        else:
                            ctxT_of(b + 1, 0, q_taken, value(b + 1, 2, 2))
                    if prep and i == 14:
                        if post:
                            ctxT_of(b + 1, 1, logits_taken, value(b - 1, 1, 1))
                        else:
                            ctxT_of(b + 1, 1, q_taken, value(b + 1, 2, 1))
                    if post and i == 15:
                        if prep:
                            count(b - 1, ctxT_taken, value(b + 1, 2, 1))
                        else:
                            count(b - 1, x1nT_taken, value(b - 1, 2, 2))
                    if prep and i == 16:
                        k_of(b + 1, 0, ctxT_taken, value(b + 1, 2, 2))
                    if prep and i == 17:
                        if post:
                            k_of(b + 1, 1, counts_taken, value(b - 1, 1, 1))
                        else:
                            k_of(b + 1, 1, ctxT_taken, value(b + 1, 2, 2))
                    if 3 <= i < UNITS + 3:
                        probsT_of(b, i - 3)
                    if 4 <= i < UNITS + 4:
                        attend(b, i - 4)
                    if prep and i in (18, 19):
                        v_of(b + 1, i - 18)

            for k in range(KD):
                xnT_of(0, k, None, 0)
            for g in range(KD):
                q_of(0, g)
            for j in range(KD):
                ctxT_of(0, j, q_taken, value(0, 2, CTX_ORDER[j] + 1))
            for g in range(KD):
                k_of(0, g, ctxT_taken, value(0, 2, 2))
            for m in range(2):
                v_of(0, m)
            pe.wait_ge(pads_ready, 2)
            body(0, False, True)
            with pe.Fori(1, B - 1) as b:
                body(b, True, True)
            body(B - 1, True, False)
            project(B - 1, 0, logits_taken, B - 1)
            project(B - 1, 1, counts_taken, B - 1)
            for k in range(KD):
                x1nT_of(B - 1, k, x1_ready, value(B - 1, 2, k + 1))
            route(B - 1)
            count(B - 1, x1nT_taken, 2 * B)

            def xdT_of(e, i, first):
                pe.wait_ge(rows_in[i], loaded(e, i))
                if not first:
                    pe.wait_ge(xdT_taken, e)
                for k in range(KD):
                    for s in range(2):
                        last = pe.transpose(ps_xdT[:, k * CAP + s * SR:k * CAP + (s + 1) * SR],
                                            q_rows[i][:, s, k * P:(k + 1) * P], ident[0:SR, 0:SR])
                last.then_inc(xdT_ready, 1)

            def loaded(e, i):
                return 8 * (e - i) + 16

            def first_product(e, i, m, first):
                if m == 0:
                    pe.wait_ge(w1_in[i], loaded(e, i))
                    pe.wait_ge(xdT_taken, e + 1)
                if not first:
                    pe.wait_ge(gelu_done, 3 * e + m - 2)
                for c, f in enumerate(M_BANKS[m]):
                    for k in range(KD):
                        last = pe.matmul(ps_hidden[m][:, c * CAP:(c + 1) * CAP], w1_sb[i][:, k, f * P:(f + 1) * P],
                                         xdT[i][:, k], start=(k == 0), stop=(k == KD - 1))
                last.then_inc(hidden_ready, 1)

            def second_product(e, i, first):
                pe.wait_ge(w2_in[i], loaded(e, i))
                if not first:
                    pe.wait_ge(yT_taken, e)
                for d in range(KD):
                    for k in range(KF):
                        if d == 0 and k in (0, 3, 6):
                            pe.wait_ge(gelu_done, 3 * e + k // 3 + 1)
                        last = pe.matmul(ps_y[:, d * CAP:(d + 1) * CAP], w2_sb[i][:, k, d * P:(d + 1) * P],
                                         hidden[:, k], start=(k == 0), stop=(k == KF - 1))
                last.then_inc(y_ready, 1)

            def yrows_of(e, first):
                pe.wait_ge(yT_taken, e + 1)
                if not first:
                    pe.wait_ge(yrows_taken, e)
                for s in range(2):
                    for d in range(KD):
                        last = pe.transpose(ps_rows[0:SR, s * D + d * P:s * D + (d + 1) * P],
                                            yT[:, d, s * SR:(s + 1) * SR], ident[:])
                last.then_inc(yrows_ready, 1)

            def expert(e, i, before_it, after_it, first, second):
                first_product(e, i, 0, first)
                if before_it:
                    yrows_of(e - 1, second)
                first_product(e, i, 1, first)
                if after_it:
                    xdT_of(e + 1, 1 - i, False)
                first_product(e, i, 2, first)
                second_product(e, i, first)

            pe.wait_ge(scores_taken, B * UNITS)
            pe.wait_ge(att_taken, B * CHUNKS)
            for i in range(2):
                pe.wait_ge(probsT_taken[i], B * UNITS // 2)
            xdT_of(0, 0, True)
            expert(0, 0, False, True, True, False)
            expert(1, 1, True, True, False, True)
            with pe.Fori(1, E // 2 - 1) as turn:
                expert(2 * turn, 0, True, True, False, False)
                expert(2 * turn + 1, 1, True, True, False, False)
            expert(E - 2, 0, True, True, False, False)
            expert(E - 1, 1, True, False, False, False)
            yrows_of(E - 1, False)


_INS = ['x', 'ctx_1024', 'mask_BxS2_bf1', 'g_xattn', 'g_ffn', 'L0_xattn_W_q', 'L0_xattn_b_q', 'L0_xattn_W_k',
        'L0_xattn_b_k', 'L0_xattn_W_v', 'L0_xattn_b_v', 'L0_xattn_W_o', 'L0_xattn_b_o', 'L0_ffn_gate_w',
        'L0_ffn_w1', 'L0_ffn_w2']
_OUTS = [((4, 512, 256), 'float32')]


def kernel(**inputs):
    import numpy as _np
    import concourse.bacc as _bacc
    from concourse import mybir as _mybir
    from concourse.bass_utils import run_bass_kernel_spmd as _run

    nc = _bacc.Bacc("TRN2", target_bir_lowering=False, num_devices=1)
    arrays, args = {}, []
    for name in _INS:
        a = _np.ascontiguousarray(inputs[name])
        if a.dtype.kind == "b":
            a = a.view(_np.uint8)
        arrays[f"in_{name}_dram"] = a
        args.append(nc.dram_tensor(f"in_{name}_dram", a.shape, _mybir.dt.from_np(a.dtype), kind="ExternalInput").ap())
    for i, (shape, dtype) in enumerate(_OUTS):
        dt = _mybir.dt.from_np(_np.dtype(dtype))
        args.append(nc.dram_tensor(f"out_{i}_dram", shape, dt, kind="ExternalOutput").ap())
    flamingo_kernel(nc, *args)
    r = _run(nc, [arrays], core_ids=[0])
    got = tuple(r.results[0][f"out_{i}_dram"] for i in range(len(_OUTS)))
    return got[0]
```

```python
from contextlib import ExitStack

import concourse.bass as bass
from concourse import mybir

F32 = mybir.dt.float32
BF16 = mybir.dt.bfloat16
U32 = mybir.dt.uint32
ALU = mybir.AluOpType
ACT = mybir.ActivationFunctionType
AX = mybir.AxisListType

P = 128
WINDOW = 64
HEADS = 16
EPS = 1e-5
MASKED = 1e30
DROPPED = 8192.0
NO_TOKEN = 1048576.0


def capacity(tokens, experts):
    cap = int(1.25 * tokens // experts)
    return max(cap + cap % 2, 4)


def flamingo_kernel(nc, x, ctx_in, mask, g_xattn, g_ffn, W_q, b_q, W_k, b_k, W_v, b_v, W_o, b_o,
                    gate_w, w1, w2, out):
    B, S, D = x.shape
    E, _, F = w1.shape
    T = S // P
    KD = D // P
    KF = F // P
    NW = S // WINDOW
    HD = D // HEADS
    HG = P // HD
    PAIRS = HG // 2
    CAP = capacity(B * S, E)
    SR = CAP // 2
    ROW = 2 * D + 2
    UNITS = 2 * KD * 4
    CHUNKS = UNITS // 4
    assert (T, KD, NW, HG, UNITS) == (4, 2, 8, 8, 16) and CAP % 32 == 0 and E % 2 == 0

    out_rows = out.rearrange("b s d -> (b s) d")
    queue = nc.dram_tensor("expert_queue", (E * CAP, ROW), F32, kind="Internal").ap()

    es = ExitStack()
    with es:
        def sb(name, shape, dt=F32):
            return es.enter_context(nc.sbuf_tensor(name, shape, dt))

        def sem(name):
            return es.enter_context(nc.semaphore(name))

        ident = sb("ident", [P, P])
        head_mask = sb("head_mask", [P, HG])
        parity_mask = sb("parity_mask", [P, 2])
        causal = sb("causal", [P, 2 * WINDOW], BF16)
        before = sb("before", [P, P], BF16)
        ones = sb("ones", [P, P], BF16)
        countdown = sb("countdown", [P, T, E])
        token_no = sb("token_no", [P, B * T])
        minus_half = sb("minus_half", [P, T])
        eps = sb("eps", [P, T])
        empty_row = sb("empty_row", [P, ROW])
        gates = sb("gates", [P, 2])
        tanh_g = sb("tanh_g", [P, 2])
        bias_qk_raw = sb("bias_qk_raw", [P, 2, KD])
        bias_q = sb("bias_q", [P, KD])
        bias_v = sb("bias_v", [P, D])
        bias_o = sb("bias_o", [P, D])
        bias_og = sb("bias_og", [P, D])
        mask_u8 = sb("mask_u8", [P, B, S], mask.dtype)
        key_valid = sb("key_valid", [P, WINDOW + S], BF16)
        mask_next = sb("mask_next", [P, 2, NW // 2, 2 * WINDOW], BF16)
        mask_now = sb("mask_now", [P, 2, NW // 2, 2 * WINDOW], BF16)
        w_raw = sb("w_raw", [P, 4, KD, D])
        gate_raw = sb("gate_raw", [E, D])
        wT = sb("wT", [P, 4, KD, D])
        gateT = sb("gateT", [P, KD, E])
        x_all = sb("x_all", [P, B, T, D])
        ctx_rows = sb("ctx_rows", [P, T, D])
        xn = sb("xn", [P, T, D])
        stats = sb("stats", [P, B, T, 6])
        mean_var = sb("mean_var", [P, B, T, 2])
        var_eps = sb("var_eps", [P, B, T])
        rstd = sb("rstd", [P, B, T])
        xnT = sb("xnT", [P, KD, S])
        ctxT = sb("ctxT", [P, KD, S])
        qT = sb("qT", [P, KD, S])
        kT = sb("kT", [P, KD, WINDOW + S])
        q_heads = sb("q_heads", [P, KD, NW, HG, WINDOW])
        v = sb("v", [P, T, D])
        v_shift = sb("v_shift", [P, T, D])
        NP_ = 4
        probs = sb("probs", [P, NP_, PAIRS, 2 * WINDOW])
        low = sb("low", [P, NP_, PAIRS])
        total = sb("total", [P, NP_, PAIRS])
        r_total = sb("r_total", [P, NP_, PAIRS])
        NT = 4
        probsT = sb("probsT", [P, NT, PAIRS, 2 * WINDOW])
        attT = sb("attT", [P, KD, S])
        rows = sb("rows", [P, T, ROW])
        stats2 = sb("stats2", [P, T, 6])
        mean_var2 = sb("mean_var2", [P, T, 2])
        var_eps2 = sb("var_eps2", [P, T])
        rstd2 = sb("rstd2", [P, T])
        x1nT = sb("x1nT", [P, KD, S])
        top = sb("top", [P, T])
        lowered = sb("lowered", [P, T, E])
        exps = sb("exps", [P, T, E])
        marks = sb("marks", [P, T, E])
        best = sb("best", [P, T])
        onehot = sb("onehot", [P, T, E], BF16)
        seen = sb("seen", [P, E], BF16)
        seen_add = sb("seen_add", [P, E])
        expsum = sb("expsum", [P, T])
        r_expsum = sb("r_expsum", [P, T])
        ranks = sb("ranks", [P, T, E])
        rank = sb("rank", [P, T])
        past = sb("past", [P, T])
        slot_f = sb("slot_f", [P, T])
        slot = sb("slot", [P, T], U32)
        w1_sb = [sb(f"w1_{i}", [P, KD, F]) for i in range(2)]
        w2_sb = [sb(f"w2_{i}", [P, KF, D]) for i in range(2)]
        q_rows = [sb(f"q_rows{i}", [SR, 2, ROW]) for i in range(2)]
        xdT = [sb(f"xdT{i}", [P, KD, CAP]) for i in range(2)]
        hidden = w_raw[:].rearrange("p w k d -> p (w k d)")[:, 0:KF * CAP].rearrange("p (k c) -> p k c", c=CAP)
        yT = sb("yT", [P, KD, CAP])
        weight = [sb(f"weight{i}", [SR, 2]) for i in range(2)]
        place = [sb(f"place{i}", [SR, 2], U32) for i in range(2)]
        resid = [sb(f"resid{i}", [SR, 2, D]) for i in range(2)]
        y_rows = [sb(f"y_rows{i}", [SR, 2, D]) for i in range(2)]

        bank = [es.enter_context(nc.psum_tensor(f"bank{i}", [P, 512], F32)) for i in range(8)]
        ps_scores, ps_probsT, ps_att, ps_misc = bank[0:2], bank[2:4], bank[4:6], bank[6:8]
        ps_hidden, ps_y, ps_xdT, ps_rows = bank[0:3], bank[3], bank[4], bank[5]

        pool_waited, dve_waited = sem("pool_waited"), sem("dve_waited")
        x_in = [sem(f"x_in{i}") for i in range(2)]
        ctx_in_s, small_in, bias_in, mask_in = sem("ctx_in"), sem("small_in"), sem("bias_in"), sem("mask_in")
        w_in = [sem(f"w_in_{w}") for w in "qkvog"]
        v_shifted = [sem("v_shifted_early"), sem("v_shifted_late")]
        prefilled, x1_out = sem("prefilled"), sem("x1_out")
        scattered = sem("scattered")
        w1_in = [sem(f"w1_in{i}") for i in range(2)]
        w2_in = [sem(f"w2_in{i}") for i in range(2)]
        rows_in = [sem(f"rows_in{i}") for i in range(2)]
        y_out = [sem(f"y_out{i}") for i in range(2)]
        const_step, consts_ready, empty_ready = sem("const_step"), sem("consts_ready"), sem("empty_ready")
        mask_step, mask_ready, mask_set = sem("mask_step"), sem("mask_ready"), sem("mask_set")
        tanh_ready, bias_ready = sem("tanh_ready"), sem("bias_ready")
        pads_ready = sem("pads_ready")
        wT_ready, wT_taken = sem("wT_ready"), [sem(f"wT_taken_{w}") for w in "qkvog"]
        x_stat, x_meanvar, x_eps, x_rstd = sem("x_stat"), sem("x_meanvar"), sem("x_eps"), sem("x_rstd")
        xn_ready, x_based = sem("xn_ready"), sem("x_based")
        xnT_ready, xnT_taken = sem("xnT_ready"), sem("xnT_taken")
        ctxT_ready, ctxT_taken = sem("ctxT_ready"), sem("ctxT_taken")
        q_ready, q_taken, q_split = sem("q_ready"), sem("q_taken"), sem("q_split")
        k_ready, k_taken = sem("k_ready"), sem("k_taken")
        v_ready, v_taken = sem("v_ready"), sem("v_taken")
        scores_ready, scores_taken = sem("scores_ready"), sem("scores_taken")
        exp_done, r_total_ready, probs_ready = sem("exp_done"), sem("r_total_ready"), sem("probs_ready")
        probsT_ready = sem("probsT_ready")
        probsT_taken = [sem("probsT_taken_dve"), sem("probsT_taken_act")]
        att_ready, att_even, att_taken = sem("att_ready"), sem("att_even"), sem("att_taken")
        o_ready, x1_ready = sem("o_ready"), sem("x1_ready")
        x1_stat, x1_meanvar, x1_eps, x1_rstd = sem("x1_stat"), sem("x1_meanvar"), sem("x1_eps"), sem("x1_rstd")
        x1n_ready = sem("x1n_ready")
        x1nT_ready, x1nT_taken = sem("x1nT_ready"), sem("x1nT_taken")
        logits_ready, logits_taken, exps_ready = sem("logits_ready"), sem("logits_taken"), sem("exps_ready")
        router_step, onehot_ready, weights_ready = sem("router_step"), sem("onehot_ready"), sem("weights_ready")
        counts_ready, counts_taken, slots_ready = sem("counts_ready"), sem("counts_taken"), sem("slots_ready")
        xdT_ready, xdT_taken, meta_taken = sem("xdT_ready"), sem("xdT_taken"), sem("meta_taken")
        hidden_ready, gelu_done = sem("hidden_ready"), sem("gelu_done")
        y_ready, yT_taken = sem("y_ready"), sem("yT_taken")
        yrows_ready, yrows_taken = sem("yrows_ready"), sem("yrows_taken")

        def value(n, per, k):
            return n * per + k

        def unit(i):
            half, g, wi = i // 8, i // 4 % 2, i % 4
            return half, g, wi, half * 4 + wi

        M_BANKS = [range(0, 3), range(3, 6), range(6, 8)]
        PT_LAG, AV_LAG = 3, 5
        SPLIT_STEPS = (7, 8, 10, 11, 12, 14)
        STATS_STEPS = (0, 6, 9)
        RANK_STEPS = 5

        block = es.enter_context(nc.Block())

        @block.sync
        def _(sp):
            def load_ctx(n):
                if not isinstance(n, int) or n > 0:
                    sp.wait_ge(ctxT_ready, value(n - 1, 2, 2))
                sp.dma_start(ctx_rows[:], ctx_in[n].rearrange("(t p) d -> p t d", p=P)).then_inc(ctx_in_s, 16)

            def shift_v(n, m):
                sp.wait_ge(v_taken, value(n, 2, m + 1))
                first, t0, t1 = max(2 * m, 1), 2 * m, 2 * m + 2
                sp.dma_start(v_shift[WINDOW:P, t0:t1, :], v[0:WINDOW, t0:t1, :]).then_inc(v_shifted[m], 16)
                sp.dma_start(v_shift[0:WINDOW, first:t1, :], v[WINDOW:P, first - 1:t1 - 1, :]).then_inc(v_shifted[m], 16)

            def store_x1(n):
                sp.wait_ge(x1_ready, value(n, 2, 2))
                sp.dma_start(out[n].rearrange("(t p) d -> p t d", p=P), rows[:, :, D:2 * D]).then_inc(x1_out, 16)

            def load_w1(e, i):
                sp.dma_start(w1_sb[i][:], w1[e].rearrange("(k p) f -> p k f", p=P)).then_inc(w1_in[i], 16)

            def load_w2(e, i):
                sp.dma_start(w2_sb[i][:], w2[e].rearrange("(k p) d -> p k d", p=P)).then_inc(w2_in[i], 16)

            def load_rows(e, i):
                sp.dma_start(q_rows[i][:], queue[bass.ts(e, CAP), :].rearrange("(s p) c -> p s c", p=SR)
                             ).then_inc(rows_in[i], 16)

            def load_w(i, w):
                sp.dma_start(w_raw[:, i], w.rearrange("(t p) d -> p t d", p=P)).then_inc(w_in[i], 16)

            sp.dma_start(x_all[:, 0], x[0].rearrange("(t p) d -> p t d", p=P)).then_inc(x_in[0], 16)
            load_w(0, W_q)
            load_w(1, W_k)
            load_ctx(0)
            load_w(2, W_v)
            sp.dma_start(mask_u8[:], mask.partition_broadcast(P)).then_inc(mask_in, 16)
            load_w(3, W_o)
            sp.dma_start(gate_raw[:], gate_w).then_inc(w_in[4], 16)
            for n in range(1, B):
                sp.dma_start(x_all[:, n], x[n].rearrange("(t p) d -> p t d", p=P)).then_inc(x_in[1], 16)
            sp.wait_ge(empty_ready, 2)
            sp.dma_start(queue.rearrange("(s p) c -> p s c", p=P),
                         empty_row[:].unsqueeze(1).to_broadcast([P, E * CAP // P, ROW])).then_inc(prefilled, 16)

            def body(b, first, last):
                if not last:
                    load_ctx(b + 1)
                shift_v(b, 0)
                shift_v(b, 1)
                if not first:
                    store_x1(b - 1)

            body(0, True, False)
            for e in range(2):
                load_w1(e, e)
                load_w2(e, e)
            with sp.Fori(1, B - 1) as b:
                body(b, False, False)
            body(B - 1, False, True)
            store_x1(B - 1)

            sp.wait_ge(scattered, 16 * T * B)
            for e in range(2):
                load_rows(e, e)

            def reload(e, i):
                sp.wait_ge(xdT_ready, e + 1)
                sp.wait_ge(meta_taken, e + 1)
                load_rows(e + 2, i)
                sp.wait_ge(hidden_ready, 3 * e + 3)
                load_w1(e + 2, i)
                sp.wait_ge(y_ready, e + 1)
                load_w2(e + 2, i)

            with sp.Fori(0, E // 2 - 1) as turn:
                reload(2 * turn, 0)
                reload(2 * turn + 1, 1)

        @block.gpsimd
        def _(pool):
            c = 0
            pool.memset(ident[:], 0.0)
            pool.memset(causal[:], 1.0)
            pool.memset(before[:], 1.0)
            pool.memset(head_mask[:], 1.0)
            pool.memset(parity_mask[:], 0.0)
            pool.memset(ones[:], 1.0)
            pool.memset(minus_half[:], -0.5)
            pool.memset(eps[:], EPS)
            pool.memset(seen[:], 0.0)
            pool.memset(empty_row[:, 0:ROW - 1], 0.0).then_inc(empty_ready, 1)
            pool.memset(empty_row[:, ROW - 1:ROW], NO_TOKEN).then_inc(empty_ready, 1)
            pool.memset(kT[:, :, 0:WINDOW], 0.0).then_inc(pads_ready, 1)
            pool.memset(v_shift[0:WINDOW, 0:1, :], 0.0).then_inc(pads_ready, 1)
            pool.memset(key_valid[:, 0:WINDOW], 0.0).then_inc(const_step, 1)
            pool.wait_ge(const_step, 1)
            pool.affine_select(out=ident[:], in_=ident[:], compare_op=ALU.not_equal, fill=1.0, base=0,
                               pattern=[[-1, P]], channel_multiplier=1)
            pool.affine_select(out=before[:], in_=before[:], compare_op=ALU.is_ge, fill=0.0, base=-1,
                               pattern=[[1, P]], channel_multiplier=-1).then_inc(const_step, 1)
            for h in range(2):
                q = slice(h * WINDOW, (h + 1) * WINDOW)
                pool.wait_ge(const_step, 2 + h)
                pool.affine_select(out=causal[q, WINDOW:], in_=causal[q, WINDOW:], compare_op=ALU.is_ge, fill=0.0,
                                   base=0, pattern=[[-1, WINDOW]], channel_multiplier=1).then_inc(const_step, 1)
            pool.wait_ge(const_step, 4)
            pool.affine_select(out=head_mask[:], in_=head_mask[:], compare_op=ALU.is_ge, fill=0.0, base=0,
                               pattern=[[-HD, HG]], channel_multiplier=1).then_inc(const_step, 1)
            pool.wait_ge(const_step, 5)
            pool.affine_select(out=head_mask[:], in_=head_mask[:], compare_op=ALU.is_ge, fill=0.0, base=HD - 1,
                               pattern=[[HD, HG]], channel_multiplier=-1).then_inc(const_step, 1)
            pool.iota(countdown[:], pattern=[[0, T], [-1, E]], base=E, channel_multiplier=0,
                      allow_small_or_imprecise_dtypes=True)
            pool.iota(token_no[:], pattern=[[P, B * T]], base=0, channel_multiplier=1,
                      allow_small_or_imprecise_dtypes=True).then_inc(consts_ready, 1)
            pool.wait_ge(const_step, 6)
            for h in range(HG):
                pool.tensor_tensor(parity_mask[:, h % 2:h % 2 + 1], parity_mask[:, h % 2:h % 2 + 1],
                                   head_mask[:, h:h + 1], ALU.add).then_inc(const_step, 1)
                pool.wait_ge(const_step, 7 + h)

            def x_rstd_of(n):
                pool.wait_ge(x_meanvar, value(n, 1, 1))
                pool.tensor_tensor(var_eps[:, n], mean_var[:, n, :, 1], eps[:], ALU.add).then_inc(x_eps, 1)
                pool.wait_ge(x_eps, value(n, 1, 1))
                pool.tensor_tensor(rstd[:, n], var_eps[:, n], minus_half[:], ALU.pow).then_inc(x_rstd, 1)

            def base_of(n):
                pool.wait_ge(xn_ready, value(n, 1, 1))
                pool.wait_ge(bias_ready, 2)
                pool.tensor_tensor(x_all[:, n], x_all[:, n], bias_og[:].unsqueeze(1).to_broadcast([P, T, D]),
                                   ALU.add).then_inc(x_based, 1)

            def norm(n, i):
                pool.wait_ge(r_total_ready, value(n, UNITS, i + 1))
                pool.tensor_tensor(probs[:, i % NP_], probs[:, i % NP_],
                                   r_total[:, i % NP_].unsqueeze(2).to_broadcast([P, PAIRS, 2 * WINDOW]),
                                   ALU.mult).then_inc(probs_ready, 1)

            def x1_rstd_of(n, m):
                tiles = slice(2 * m, 2 * m + 2)
                pool.wait_ge(x1_meanvar, value(n, 2, m + 1))
                pool.tensor_tensor(var_eps2[:, tiles], mean_var2[:, tiles, 1], eps[:, tiles], ALU.add).then_inc(x1_eps, 1)
                pool.wait_ge(x1_eps, value(n, 2, m + 1))
                pool.tensor_tensor(rstd2[:, tiles], var_eps2[:, tiles], minus_half[:, tiles], ALU.pow
                                   ).then_inc(x1_rstd, 1)

            def scatter(n):
                pool.wait_ge(prefilled, 16)
                pool.wait_ge(slots_ready, value(n, 1, 1))
                pool.wait_ge(weights_ready, value(n, 2, 2))
                pool.wait_ge(x1n_ready, value(n, 2, 2))
                pool.sem_inc(pool_waited, 1)
                for t in range(T):
                    pool.indirect_dma_start(out=queue, out_offset=bass.IndirectOffsetOnAxis(ap=slot[:, t:t + 1], axis=0),
                                            in_=rows[:, t, :], in_offset=None, bounds_check=E * CAP - 1,
                                            oob_is_err=False).then_inc(scattered, 16)

            def body(b, first, last):
                for i in range(UNITS + (1 if last else 0)):
                    if i > 0 or not first:
                        norm(b, i - 1)
                    if first and i in STATS_STEPS:
                        x_rstd_of(1 + STATS_STEPS.index(i))
                    if i == 3 and not last:
                        base_of(b + 1)
                    if i == 8 and not first:
                        x1_rstd_of(b - 1, 0)
                        x1_rstd_of(b - 1, 1)
                    if i == 15 and not first:
                        scatter(b - 1)

            x_rstd_of(0)
            base_of(0)
            body(0, True, False)
            with pool.Fori(1, B - 1) as b:
                body(b, False, False)
            body(B - 1, False, True)
            x1_rstd_of(B - 1, 0)
            x1_rstd_of(B - 1, 1)
            scatter(B - 1)

            def place_rows(e, i):
                pool.wait_ge(x1_out, 16 * B)
                pool.wait_ge(yrows_taken, e + 1)
                pool.sem_inc(pool_waited, 1)
                for s in range(2):
                    pool.indirect_dma_start(out=out_rows,
                                            out_offset=bass.IndirectOffsetOnAxis(ap=place[i][:, s:s + 1], axis=0),
                                            in_=y_rows[i][:, s, :], in_offset=None, bounds_check=B * S - 1,
                                            oob_is_err=False).then_inc(y_out[i], 16)

            with pool.Fori(0, E // 2) as turn:
                place_rows(2 * turn, 0)
                place_rows(2 * turn + 1, 1)
            for i in range(2):
                pool.wait_ge(y_out[i], 16 * E)

        @block.scalar
        def _(act):
            for i, b in enumerate((b_q, b_k)):
                act.dma_start(bias_qk_raw[:, i], b.rearrange("(g p) -> p g", p=P),
                              allow_slow_non_contiguous=True).then_inc(bias_in, 16)
            act.dma_start(gates[:, 0:1], g_xattn.partition_broadcast(P)).then_inc(small_in, 16)
            act.dma_start(gates[:, 1:2], g_ffn.partition_broadcast(P)).then_inc(small_in, 16)
            act.dma_start(bias_v[:], b_v.partition_broadcast(P)).then_inc(small_in, 16)
            act.dma_start(bias_o[:], b_o.partition_broadcast(P)).then_inc(small_in, 16)

            def take_wT(i, step):
                act.wait_ge(wT_ready, step)
                act.activation(wT[:, i], bank[i][:].rearrange("p (k d) -> p k d", k=KD), ACT.Copy).then_inc(wT_taken[i], 1)

            def take_xnT(n, k):
                act.wait_ge(xnT_ready, value(n, 2, k + 1))
                act.activation(xnT[:, k], ps_misc[k][:], ACT.Copy).then_inc(xnT_taken, 1)

            def take_q(n, g):
                act.wait_ge(q_ready, value(n, 2, g + 1))
                if not isinstance(n, int) or n > 0:
                    act.wait_ge(q_split, value(n - 1, 2 * CHUNKS, 2 * CHUNKS))
                act.activation(qT[:, g], ps_misc[g][:], ACT.Identity, bias=bias_q[:, g:g + 1],
                               scale=-float(HD) ** -0.5).then_inc(q_taken, 1)

            def take_ctxT(n, k):
                act.wait_ge(ctxT_ready, value(n, 2, k + 1))
                act.wait_ge(v_ready, value(n - 1, 2, 2))
                act.activation(ctxT[:, k], ps_misc[0][:], ACT.Copy).then_inc(ctxT_taken, 1)

            def take_k(n, g):
                act.wait_ge(k_ready, value(n, 2, g + 1))
                if not isinstance(n, int) or n > 0:
                    act.wait_ge(scores_ready, value(n - 1, UNITS, UNITS - 4 + 4 * g))
                act.activation(kT[:, g, WINDOW:], ps_misc[g][:], ACT.Identity,
                               bias=bias_qk_raw[:, 1, g:g + 1]).then_inc(k_taken, 1)

            def exp(n, i):
                act.wait_ge(scores_taken, value(n, UNITS, i + 1))
                for j in range(PAIRS):
                    last = act.activation(probs[:, i % NP_, j], probs[:, i % NP_, j], ACT.Exp, scale=-1.0,
                                          bias=low[:, i % NP_, j:j + 1], accum_out=total[:, i % NP_, j:j + 1])
                last.then_inc(exp_done, 1)

            def take_probsT(n, i):
                act.wait_ge(probsT_ready, value(n, UNITS, i + 1))
                if i >= NT or not isinstance(n, int) or n > 0:
                    act.wait_ge(att_ready, value(n, UNITS, i - NT + 1))
                act.activation(probsT[:, i % NT], ps_probsT[i % 2][:].rearrange("p (j q) -> p j q", j=PAIRS),
                               ACT.Copy).then_inc(probsT_taken[1], 1)

            def take_x1nT(n, k):
                act.wait_ge(x1nT_ready, value(n, 2, k + 1))
                act.activation(x1nT[:, k], ps_misc[1 - k][:], ACT.Copy).then_inc(x1nT_taken, 1)

            def exp_logits(n):
                act.wait_ge(logits_taken, value(n, 1, 1))
                act.activation(exps[:], lowered[:], ACT.Exp).then_inc(exps_ready, 1)

            def body(b, first, last):
                for i in range(UNITS + (PT_LAG if last else 0)):
                    if i == 2:
                        take_k(b, 1)
                    if first and i == 1:
                        take_wT(3, 4)
                    if not last and i in (3, 4):
                        take_xnT(b + 1, i - 3)
                    if not last and i in (6, 7):
                        take_q(b + 1, i - 6)
                    if not last and i in (9, 10):
                        take_ctxT(b + 1, i - 9)
                    if not first and i in (11, 12):
                        take_x1nT(b - 1, i - 11)
                    if not last and i == 14:
                        take_k(b + 1, 0)
                    if not first and i == 15:
                        exp_logits(b - 1)
                    if i < UNITS:
                        exp(b, i)
                    if (i >= PT_LAG or not first) and (i - PT_LAG) % 2 == 1:
                        take_probsT(b, i - PT_LAG)

            take_wT(0, 1)
            take_wT(1, 2)
            for k in range(KD):
                take_xnT(0, k)
            act.wait_ge(bias_in, 2 * 16)
            act.wait_ge(bias_ready, 1)
            for g in range(KD):
                take_q(0, g)
            take_k(0, 0)
            act.wait_ge(small_in, 4 * 16)
            act.activation(tanh_g[:], gates[:], ACT.Tanh).then_inc(tanh_ready, 1)
            body(0, True, False)
            with act.Fori(1, B - 1) as b:
                body(b, False, False)
            body(B - 1, False, True)
            for k in range(KD):
                take_x1nT(B - 1, k)
            exp_logits(B - 1)

            def gelu(e, first):
                for m, ms in enumerate(M_BANKS):
                    act.wait_ge(hidden_ready, 3 * e + m + 1)
                    if not first:
                        act.wait_ge(y_ready, e)
                    n = len(ms) * CAP
                    act.activation(hidden[:, ms[0]:ms[-1] + 1, :], ps_hidden[m][:, 0:n].rearrange("p (m c) -> p m c", c=CAP),
                                   ACT.Gelu_apprx_tanh).then_inc(gelu_done, 1)

            gelu(0, True)
            gelu(1, False)
            with act.Fori(1, E // 2) as turn:
                gelu(2 * turn, False)
                gelu(2 * turn + 1, False)

        @block.vector
        def _(dve):
            def x_stats(n):
                if n == 0:
                    dve.wait_ge(x_in[0], 16)
                else:
                    dve.wait_ge(x_in[1], 16 * (B - 1))
                for t in range(T):
                    last = dve.bn_stats(stats[:, n, t], x_all[:, n, t])
                last.then_inc(x_stat, 1)
                dve.wait_ge(x_stat, n + 1)
                for t in range(T):
                    last = dve.bn_aggr(mean_var[:, n, t], stats[:, n, t])
                last.then_inc(x_meanvar, 1)

            def x_norm(n):
                dve.wait_ge(x_rstd, value(n, 1, 1))
                if not isinstance(n, int) or n > 0:
                    dve.wait_ge(xnT_ready, value(n - 1, 2, 2))
                for t in range(T):
                    last = dve.tensor_scalar(xn[:, t], x_all[:, n, t], mean_var[:, n, t, 0:1], rstd[:, n, t:t + 1],
                                             ALU.subtract, ALU.mult)
                last.then_inc(xn_ready, 1)

            def mask_of(n):
                if not isinstance(n, int) or n > 0:
                    dve.wait_ge(mask_set, value(n, 1, 0))
                dve.tensor_copy(key_valid[:, WINDOW:], mask_u8[:, n]).then_inc(mask_step, 1)
                dve.wait_ge(mask_step, value(n, 1, 1))
                for e in range(2):
                    keys = key_valid[:, e * WINDOW:e * WINDOW + S].rearrange("p (w k) -> p w k", k=2 * WINDOW)
                    dve.tensor_tensor(mask_next[:, e], keys,
                                      causal[:].unsqueeze(1).to_broadcast([P, NW // 2, 2 * WINDOW]),
                                      ALU.mult).then_inc(mask_ready, 1)

            def take_v(n, m):
                dve.wait_ge(v_ready, value(n, 2, m + 1))
                if not isinstance(n, int) or n > 0:
                    dve.wait_ge(att_ready, value(n - 1, UNITS, UNITS // 2 * (m + 1)))
                    for part in v_shifted:
                        dve.wait_ge(part, 32 * n)
                dve.tensor_tensor(v[:, 2 * m:2 * m + 2], ps_misc[m][:].rearrange("p (t d) -> p t d", d=D),
                                  bias_v[:].unsqueeze(1).to_broadcast([P, 2, D]), ALU.add).then_inc(v_taken, 1)

            def low_of(n, i):
                _, _, _, w = unit(i)
                dve.wait_ge(scores_ready, value(n, UNITS, i + 1))
                if i >= NP_:
                    dve.wait_ge(probsT_ready, value(n, UNITS, i - NP_ + 1))
                elif not isinstance(n, int) or n > 0:
                    dve.wait_ge(probsT_ready, value(n - 1, UNITS, UNITS + i - NP_ + 1))
                if i == 0:
                    dve.wait_ge(mask_ready, value(n, 2, 2))
                    if not isinstance(n, int) or n > 0:
                        dve.wait_ge(scores_taken, value(n - 1, UNITS, UNITS))
                    dve.tensor_scalar(mask_now[:], mask_next[:], -MASKED, MASKED, ALU.mult, ALU.add
                                      ).then_inc(mask_set, 1)
                    dve.wait_ge(mask_set, value(n, 1, 1))
                dve.sem_inc(dve_waited, 1)
                for j in range(PAIRS):
                    last = dve.tensor_tensor_reduce(
                        probs[:, i % NP_, j], ps_scores[i % 2][:, j * P:(j + 1) * P], mask_now[:, w % 2, w // 2],
                        1.0, 3.0e38, ALU.add, ALU.min, low[:, i % NP_, j:j + 1])
                last.then_inc(scores_taken, 1)

            def r_total_of(n, i):
                dve.wait_ge(exp_done, value(n, UNITS, i + 1))
                dve.reciprocal(r_total[:, i % NP_], total[:, i % NP_]).then_inc(r_total_ready, 1)

            def take_probsT(n, i):
                dve.wait_ge(probsT_ready, value(n, UNITS, i + 1))
                if i >= NT or not isinstance(n, int) or n > 0:
                    dve.wait_ge(att_ready, value(n, UNITS, i - NT + 1))
                dve.tensor_copy(probsT[:, i % NT], ps_probsT[i % 2][:].rearrange("p (j q) -> p j q", j=PAIRS)
                                ).then_inc(probsT_taken[0], 1)

            def take_att(n, c):
                half, g, _, _ = unit(4 * c)
                dve.wait_ge(att_ready, value(n, UNITS, 4 * c + 4))
                if not isinstance(n, int) or n > 0:
                    dve.wait_ge(o_ready, value(n - 1, 2, half + 1))
                src = ps_att[c % 2][:].rearrange("p (w e q) -> p w e q", w=4, e=2)
                dst = attT[:, g, half * 4 * WINDOW:(half + 1) * 4 * WINDOW].rearrange("p (w q) -> p w q", q=WINDOW)
                dve.tensor_scalar(dst, src[:, :, 0], parity_mask[:, 0:1], None, ALU.mult).then_inc(att_even, 1)
                dve.wait_ge(att_even, value(n, CHUNKS, c + 1))
                dve.scalar_tensor_tensor(dst, src[:, :, 1], parity_mask[:, 1:2], dst, ALU.mult, ALU.add
                                         ).then_inc(att_taken, 1)

            def split_q(n, part):
                c, h0 = part // 2, part % 2 * 4
                half, g, _, _ = unit(4 * c)
                if part % 2 == 0:
                    dve.wait_ge(q_taken, value(n, 2, g + 1))
                    if not isinstance(n, int) or n > 0:
                        dve.wait_ge(scores_ready, value(n - 1, UNITS, 4 * c + 4))
                src = qT[:, g, half * 4 * WINDOW:(half + 1) * 4 * WINDOW].rearrange("p (w q) -> p w q", q=WINDOW)
                for h in range(h0, h0 + 4):
                    last = dve.tensor_scalar(q_heads[:, g, half * 4:half * 4 + 4, h, :], src,
                                              head_mask[:, h:h + 1], None, ALU.mult)
                last.then_inc(q_split, 1)

            def x1_of(n, k):
                dve.wait_ge(o_ready, value(n, 2, k + 1))
                dve.wait_ge(x_based, value(n, 1, 1))
                if not isinstance(n, int) or n > 0:
                    dve.wait_ge(x1_out, 16 * n)
                    dve.wait_ge(scattered, 16 * T * n)
                dve.scalar_tensor_tensor(rows[:, 2 * k:2 * k + 2, D:2 * D],
                                         ps_misc[k][:].rearrange("p (t d) -> p t d", d=D), tanh_g[:, 0:1],
                                         x_all[:, n, 2 * k:2 * k + 2], ALU.mult, ALU.add).then_inc(x1_ready, 1)

            def x1_stats(n, m):
                dve.wait_ge(x1_ready, value(n, 2, m + 1))
                for t in range(2 * m, 2 * m + 2):
                    last = dve.bn_stats(stats2[:, t], rows[:, t, D:2 * D])
                last.then_inc(x1_stat, 1)
                dve.wait_ge(x1_stat, value(n, 2, m + 1))
                dve.sem_inc(dve_waited, 1)
                for t in range(2 * m, 2 * m + 2):
                    last = dve.bn_aggr(mean_var2[:, t], stats2[:, t])
                last.then_inc(x1_meanvar, 1)

            def x1_norm(n, m):
                dve.wait_ge(x1_rstd, value(n, 2, m + 1))
                for t in range(2 * m, 2 * m + 2):
                    last = dve.tensor_scalar(rows[:, t, 0:D], rows[:, t, D:2 * D], mean_var2[:, t, 0:1],
                                             rstd2[:, t:t + 1], ALU.subtract, ALU.mult)
                last.then_inc(x1n_ready, 1)

            def choose(n):
                def done(k):
                    dve.wait_ge(router_step, value(n, RANK_STEPS + 3, k))
                dve.wait_ge(logits_ready, value(n, 1, 1))
                logits = ps_misc[1][:, 0:T * E].rearrange("p (t e) -> p t e", e=E)
                dve.tensor_reduce(top[:], logits, AX.X, ALU.max).then_inc(router_step, 1)
                done(1)
                dve.tensor_tensor(lowered[:], logits, top[:].unsqueeze(2).to_broadcast([P, T, E]), ALU.subtract
                                  ).then_inc(logits_taken, 1)
                dve.wait_ge(logits_taken, value(n, 1, 1))
                dve.scalar_tensor_tensor(marks[:], lowered[:], 0.0, countdown[:], ALU.is_ge, ALU.mult
                                         ).then_inc(router_step, 1)
                done(2)
                dve.tensor_reduce(best[:], marks[:], AX.X, ALU.max).then_inc(router_step, 1)
                done(3)
                dve.tensor_tensor(onehot[:], marks[:], best[:].unsqueeze(2).to_broadcast([P, T, E]), ALU.is_equal
                                  ).then_inc(onehot_ready, 1)

            def weights_of(n):
                def done(k):
                    dve.wait_ge(router_step, value(n, RANK_STEPS + 3, 3 + k))
                dve.wait_ge(exps_ready, value(n, 1, 1))
                dve.tensor_reduce(expsum[:], exps[:], AX.X, ALU.add).then_inc(router_step, 1)
                done(1)
                dve.reciprocal(r_expsum[:], expsum[:]).then_inc(router_step, 1)
                done(2)
                dve.tensor_scalar(rows[:, :, 2 * D], r_expsum[:], tanh_g[:, 1:2], None, ALU.mult
                                  ).then_inc(weights_ready, 1)
                dve.tensor_copy(rows[:, :, 2 * D + 1], token_no[:, bass.ts(n, T)]).then_inc(weights_ready, 1)

            def rank_of(n):
                def done(k):
                    dve.wait_ge(router_step, value(n, RANK_STEPS + 3, 3 + k))
                dve.wait_ge(counts_ready, value(n, 1, 1))
                counts = ps_misc[1][:, 0:T * E].rearrange("p (t e) -> p t e", e=E)
                dve.tensor_tensor(ranks[:], counts, onehot[:], ALU.mult).then_inc(counts_taken, 1)
                dve.wait_ge(counts_taken, value(n, 1, 1))
                dve.tensor_reduce(rank[:], ranks[:], AX.X, ALU.add).then_inc(router_step, 1)
                dve.tensor_reduce(seen_add[:], onehot[:].rearrange("p t e -> p e t"), AX.X, ALU.add
                                  ).then_inc(router_step, 1)
                done(4)
                dve.tensor_tensor(seen[:], seen[:], seen_add[:], ALU.add)
                dve.tensor_scalar(past[:], rank[:], float(CAP), DROPPED, ALU.is_ge, ALU.mult)
                dve.scalar_tensor_tensor(slot_f[:], best[:], -float(CAP), rank[:], ALU.mult, ALU.add
                                         ).then_inc(router_step, 1)
                done(5)
                dve.scalar_tensor_tensor(slot[:], slot_f[:], float(E * CAP), past[:], ALU.add, ALU.add
                                         ).then_inc(slots_ready, 1)

            def body(b, first, last):
                for i in range(UNITS + (6 if last else 0)):
                    if i < UNITS:
                        low_of(b, i)
                    if (i >= 1 or not first) and i - 1 < UNITS:
                        r_total_of(b, i - 1)
                    if (i >= PT_LAG or not first) and i - PT_LAG < UNITS and (i - PT_LAG) % 2 == 0:
                        take_probsT(b, i - PT_LAG)
                    if not first and i in (1, 5):
                        take_att(b - 1, 2 + i // 4)
                    if i in (9, 13, 17, 21):
                        take_att(b, (i - 9) // 4)
                    if first and i == 0:
                        dve.wait_ge(small_in, 4 * 16)
                        dve.wait_ge(tanh_ready, 1)
                        dve.tensor_scalar(bias_og[:], bias_o[:], tanh_g[:, 0:1], None, ALU.mult).then_inc(bias_ready, 1)
                    if first and i == 2:
                        dve.wait_ge(wT_ready, 5)
                        dve.tensor_copy(gateT[:], bank[5][:, 0:KD * E].rearrange("p (k e) -> p k e", e=E)
                                        ).then_inc(wT_taken[4], 1)
                    if i == 0:
                        take_v(b, 0)
                    if first and i < 6:
                        split_q(b, 2 + i)
                    if not first and i in (2, 3):
                        split_q(b, 4 + i)
                    if not last and i in SPLIT_STEPS:
                        split_q(b + 1, SPLIT_STEPS.index(i))
                    if first and i in STATS_STEPS:
                        x_stats(1 + STATS_STEPS.index(i))
                    if not last and i == (1 if first else 0):
                        x_norm(b + 1)
                    if not last and i == 4:
                        mask_of(b + 1)
                    if not first and i in (6, 7):
                        x1_of(b - 1, i - 6)
                        x1_stats(b - 1, i - 6)
                    if i == 9:
                        take_v(b, 1)
                    if not first and i == 9:
                        x1_norm(b - 1, 0)
                        x1_norm(b - 1, 1)
                    if not first and i == 13:
                        choose(b - 1)
                    if not first and i == 15:
                        weights_of(b - 1)
                        rank_of(b - 1)

            x_stats(0)
            x_norm(0)
            dve.wait_ge(bias_in, 2 * 16)
            dve.tensor_scalar(bias_q[:], bias_qk_raw[:, 0], -float(HD) ** -0.5, None, ALU.mult).then_inc(bias_ready, 1)
            for k in range(KD):
                dve.wait_ge(ctxT_ready, k + 1)
                dve.tensor_copy(ctxT[:, k], bank[4 + k][:]).then_inc(ctxT_taken, 1)
            dve.wait_ge(wT_ready, 3)
            dve.tensor_copy(wT[:, 2], bank[2][:].rearrange("p (k d) -> p k d", k=KD)).then_inc(wT_taken[2], 1)
            for part in range(2):
                split_q(0, part)
            dve.wait_ge(mask_in, 16)
            dve.wait_ge(consts_ready, 1)
            mask_of(0)
            body(0, True, False)
            with dve.Fori(1, B - 1) as b:
                body(b, False, False)
            body(B - 1, False, True)
            for m in range(2):
                x1_of(B - 1, m)
                x1_stats(B - 1, m)
                x1_norm(B - 1, m)
            choose(B - 1)
            weights_of(B - 1)
            rank_of(B - 1)

            def take_xd(e, i, first):
                dve.wait_ge(xdT_ready, e + 1)
                if not first:
                    dve.wait_ge(hidden_ready, 3 * e - 3)
                    dve.wait_ge(y_out[i], 16 * (e - i))
                dve.tensor_copy(xdT[i][:], ps_xdT[:, 0:KD * CAP].rearrange("p (k c) -> p k c", c=CAP)
                                ).then_inc(xdT_taken, 1)
                dve.tensor_copy(place[i][:], q_rows[i][:, :, 2 * D + 1])
                dve.tensor_copy(weight[i][:], q_rows[i][:, :, 2 * D])
                dve.tensor_copy(resid[i][:], q_rows[i][:, :, D:2 * D]).then_inc(meta_taken, 1)

            def take_yT(e):
                dve.wait_ge(y_ready, e + 1)
                dve.tensor_copy(yT[:], ps_y[:, 0:KD * CAP].rearrange("p (k c) -> p k c", c=CAP)).then_inc(yT_taken, 1)

            def take_yrows(e, i):
                dve.wait_ge(yrows_ready, e + 1)
                dve.wait_ge(meta_taken, e + 1)
                for s in range(2):
                    last = dve.scalar_tensor_tensor(y_rows[i][:, s], ps_rows[0:SR, s * D:(s + 1) * D],
                                                    weight[i][:, s:s + 1], resid[i][:, s], ALU.mult, ALU.add)
                last.then_inc(yrows_taken, 1)

            def expert(e, i, before_it, after_it, first):
                if before_it:
                    take_yrows(e - 1, 1 - i)
                if after_it:
                    take_xd(e + 1, 1 - i, first)
                take_yT(e)

            take_xd(0, 0, True)
            expert(0, 0, False, True, True)
            expert(1, 1, True, True, False)
            with dve.Fori(1, E // 2 - 1) as turn:
                expert(2 * turn, 0, True, True, False)
                expert(2 * turn + 1, 1, True, True, False)
            expert(E - 2, 0, True, True, False)
            expert(E - 1, 1, True, False, False)
            take_yrows(E - 1, 1)

        @block.tensor
        def _(pe):
            def wT_of(i):
                pe.wait_ge(w_in[i], 16)
                for k in range(KD):
                    for d in range(KD):
                        last = pe.transpose(bank[i][:, k * D + d * P:k * D + (d + 1) * P],
                                            w_raw[:, i, d, k * P:(k + 1) * P], ident[:])
                last.then_inc(wT_ready, 1)

            def xnT_of(n, k, free=None, least=0):
                pe.wait_ge(xn_ready, value(n, 1, 1))
                if free is not None:
                    pe.wait_ge(free, least)
                for t in range(T):
                    last = pe.transpose(ps_misc[k][:, t * P:(t + 1) * P], xn[:, t, k * P:(k + 1) * P], ident[:])
                last.then_inc(xnT_ready, 1)

            def ctxT_of(n, k, ps, free=None, least=0):
                pe.wait_ge(ctx_in_s, 16 * (n + 1))
                if free is not None:
                    pe.wait_ge(free, least)
                for t in range(T):
                    last = pe.transpose(ps[:, t * P:(t + 1) * P], ctx_rows[:, t, k * P:(k + 1) * P], ident[:])
                last.then_inc(ctxT_ready, 1)

            def q_of(n, g):
                pe.wait_ge(xnT_taken, value(n, 2, 2))
                for k in range(KD):
                    last = pe.matmul(ps_misc[g][:], wT[:, 0, k, g * P:(g + 1) * P], xnT[:, k], start=(k == 0),
                                     stop=(k == KD - 1))
                last.then_inc(q_ready, 1)

            def k_of(n, g, free, least):
                pe.wait_ge(free, least)
                pe.wait_ge(ctxT_taken, value(n, 2, 2))
                for k in range(KD):
                    last = pe.matmul(ps_misc[g][:], wT[:, 1, k, g * P:(g + 1) * P], ctxT[:, k], start=(k == 0),
                                     stop=(k == KD - 1))
                last.then_inc(k_ready, 1)

            def v_of(n, m, free, least):
                pe.wait_ge(free, least)
                for t in range(2 * m, 2 * m + 2):
                    for k in range(KD):
                        last = pe.matmul(ps_misc[m][:, t % 2 * D:(t % 2 + 1) * D], ctxT[:, k, t * P:(t + 1) * P],
                                         wT[:, 2, k], start=(k == 0), stop=(k == KD - 1))
                last.then_inc(v_ready, 1)

            def scores(n, i):
                _, g, _, w = unit(i)
                if i % 4 == 0:
                    pe.wait_ge(q_split, value(n, 2 * CHUNKS, 2 * (i // 4) + 2))
                if i in (0, 4):
                    pe.wait_ge(k_taken, value(n, 2, 1 + i // 4))
                if i >= 2:
                    pe.wait_ge(scores_taken, value(n, UNITS, i - 1))
                elif not isinstance(n, int) or n > 0:
                    pe.wait_ge(scores_taken, value(n - 1, UNITS, UNITS + i - 1))
                for j in range(PAIRS):
                    last = pe.matmul(ps_scores[i % 2][:, j * P:(j + 1) * P],
                                     q_heads[:, g, w, 2 * j:2 * j + 2, :],
                                     kT[:, g, w * WINDOW:w * WINDOW + 2 * WINDOW], start=True, stop=True)
                last.then_inc(scores_ready, 1)

            def probsT_of(n, i):
                pe.wait_ge(probs_ready, value(n, UNITS, i + 1))
                if i >= 2 or not isinstance(n, int) or n > 0:
                    pe.wait_ge(probsT_taken[i % 2], value(n, UNITS // 2, i // 2))
                for j in range(PAIRS):
                    last = pe.transpose(ps_probsT[i % 2][:, j * P:(j + 1) * P], probs[:, i % NP_, j], ident[:])
                last.then_inc(probsT_ready, 1)

            def attend(n, i):
                _, g, wi, w = unit(i % UNITS)
                c = i // 4
                pe.wait_ge(probsT_taken[i % 2], value(n, UNITS // 2, i // 2 + 1))
                if i in (0, 8):
                    pe.wait_ge(v_taken, value(n, 2, 1 + i // 8))
                    pe.wait_ge(v_shifted[i // 8], 32 * (n + 1))
                if wi == 0 and (c >= 2 or not isinstance(n, int) or n > 0):
                    pe.wait_ge(att_taken, value(n, CHUNKS, c - 1))
                src = v if w % 2 else v_shift
                for j in range(PAIRS):
                    last = pe.matmul(ps_att[c % 2][j * 32:(j + 1) * 32, wi * P:(wi + 1) * P],
                                     src[:, w // 2, g * P + j * 32:g * P + (j + 1) * 32], probsT[:, i % NT, j],
                                     start=True, stop=True)
                last.then_inc(att_ready, 1)

            def project(n, m, free, least):
                pe.wait_ge(free, least)
                pe.wait_ge(att_taken, value(n, CHUNKS, CHUNKS // 2 * (m + 1)))
                for t in range(2 * m, 2 * m + 2):
                    for g in range(KD):
                        last = pe.matmul(ps_misc[m][:, t % 2 * D:(t % 2 + 1) * D], attT[:, g, t * P:(t + 1) * P],
                                         wT[:, 3, g], start=(g == 0), stop=(g == KD - 1))
                last.then_inc(o_ready, 1)

            def x1nT_of(n, k, free, least):
                pe.wait_ge(free, least)
                for t in range(T):
                    if k == 0 and t % 2 == 0:
                        pe.wait_ge(x1n_ready, value(n, 2, 1 + t // 2))
                    last = pe.transpose(ps_misc[1 - k][:, t * P:(t + 1) * P], rows[:, t, k * P:(k + 1) * P], ident[:])
                last.then_inc(x1nT_ready, 1)

            def route(n):
                pe.wait_ge(x1nT_taken, value(n, 2, 2))
                for t in range(T):
                    for k in range(KD):
                        last = pe.matmul(ps_misc[1][:, t * E:(t + 1) * E], x1nT[:, k, t * P:(t + 1) * P],
                                         gateT[:, k], start=(k == 0), stop=(k == KD - 1))
                last.then_inc(logits_ready, 1)

            def count(n):
                pe.wait_ge(onehot_ready, value(n, 1, 1))
                if not isinstance(n, int) or n > 0:
                    pe.wait_ge(slots_ready, value(n - 1, 1, 1))
                bank_ = ps_misc[1][:, 0:T * E]
                pe.matmul(bank_, ones[:], seen[:].unsqueeze(1).to_broadcast([P, T, E]), start=True, stop=False,
                          skip_group_check=True)
                for t in range(T - 1):
                    pe.matmul(bank_[:, (t + 1) * E:], ones[:],
                              onehot[:, t:t + 1].to_broadcast([P, T - 1 - t, E]), start=False, stop=False,
                              skip_group_check=True)
                pe.matmul(bank_, before[:], onehot[:], start=False, stop=True, skip_group_check=True
                          ).then_inc(counts_ready, 1)

            def body(b, first, last):
                for i in range(UNITS + (AV_LAG if last else 0)):
                    if i < UNITS:
                        scores(b, i)
                    if first and i == 0:
                        v_of(b, 0, k_taken, 1)
                    if i == 1:
                        k_of(b, 1, v_taken, value(b, 2, 1))
                    if first and i == 1:
                        wT_of(3)
                        gateT_of(bank[5])
                    if not last and i == 2:
                        xnT_of(b + 1, 0, v_taken, value(b, 2, 1))
                    if not last and i == 3:
                        xnT_of(b + 1, 1, k_taken, value(b, 2, 2))
                    if not last and i == 5:
                        q_of(b + 1, 0)
                        q_of(b + 1, 1)
                    if not first and i in (6, 7):
                        if last:
                            project(b - 1, i - 6, (v_taken, k_taken)[i - 6], value(b, 2, i - 5))
                        else:
                            project(b - 1, i - 6, q_taken, value(b + 1, 2, i - 5))
                    if not last and i == 8:
                        if first:
                            ctxT_of(b + 1, 0, ps_misc[0], q_taken, value(b + 1, 2, 1))
                        else:
                            ctxT_of(b + 1, 0, ps_misc[0], x1_ready, value(b - 1, 2, 1))
                    if not last and i == 13:
                        if first:
                            k_of(b + 1, 0, ctxT_taken, value(b + 1, 2, 2))
                        else:
                            k_of(b + 1, 0, x1nT_taken, value(b - 1, 2, 2))
                    if not first and i == 13:
                        route(b - 1)
                    if first and i == PT_LAG + 1:
                        pe.wait_ge(wT_taken[3], 1)
                    if (i >= PT_LAG or not first) and i - PT_LAG < UNITS:
                        probsT_of(b, i - PT_LAG)
                    if first and i == AV_LAG + 4:
                        pe.wait_ge(wT_taken[4], 1)
                    if i >= AV_LAG or not first:
                        attend(b, i - AV_LAG)
                    if i == 8:
                        if first:
                            v_of(b, 1, q_taken, value(b + 1, 2, 2))
                        else:
                            v_of(b, 1, x1_ready, value(b - 1, 2, 2))
                    if not last and i == 9:
                        ctxT_of(b + 1, 1, ps_misc[0], ctxT_taken, value(b + 1, 2, 1))
                    if not first and i == 10:
                        x1nT_of(b - 1, 0, v_taken, value(b, 2, 2))
                    if not first and i == 11:
                        if last:
                            x1nT_of(b - 1, 1, x1_ready, value(b - 1, 2, 1))
                        else:
                            x1nT_of(b - 1, 1, ctxT_taken, value(b + 1, 2, 2))
                    if not first and i == 14:
                        count(b - 1)
                    if not last and i == 15:
                        v_of(b + 1, 0, k_taken, value(b + 1, 2, 1))
                    if last and i == UNITS:
                        project(b, 0, x1nT_taken, value(b - 1, 2, 2))

            def gateT_of(ps):
                pe.wait_ge(w_in[4], 16)
                for k in range(KD):
                    last = pe.transpose(ps[:, k * E:(k + 1) * E], gate_raw[:, k * P:(k + 1) * P], ident[0:E, 0:E])
                last.then_inc(wT_ready, 1)

            pe.wait_ge(consts_ready, 1)
            wT_of(0)
            wT_of(1)
            for k in range(KD):
                xnT_of(0, k)
            for k in range(KD):
                ctxT_of(0, k, bank[4 + k])
            pe.wait_ge(wT_taken[0], 1)
            for g in range(KD):
                q_of(0, g)
            pe.wait_ge(wT_taken[1], 1)
            k_of(0, 0, q_taken, 1)
            wT_of(2)
            pe.wait_ge(wT_taken[2], 1)
            pe.wait_ge(pads_ready, 2)
            body(0, True, False)
            with pe.Fori(1, B - 1) as b:
                body(b, False, False)
            body(B - 1, False, True)
            project(B - 1, 1, counts_taken, B - 1)
            for k in range(KD):
                x1nT_of(B - 1, k, x1_ready, value(B - 1, 2, 2 - k))
            route(B - 1)
            count(B - 1)

            def xdT_of(e, i, first):
                pe.wait_ge(rows_in[i], loaded(e, i))
                if not first:
                    pe.wait_ge(xdT_taken, e)
                for k in range(KD):
                    for s in range(2):
                        last = pe.transpose(ps_xdT[:, k * CAP + s * SR:k * CAP + (s + 1) * SR],
                                            q_rows[i][:, s, k * P:(k + 1) * P], ident[0:SR, 0:SR])
                last.then_inc(xdT_ready, 1)

            def loaded(e, i):
                return 8 * (e - i) + 16

            def first_product(e, i, m, first):
                if m == 0:
                    pe.wait_ge(w1_in[i], loaded(e, i))
                    pe.wait_ge(xdT_taken, e + 1)
                if not first:
                    pe.wait_ge(gelu_done, 3 * e + m - 2)
                for c, f in enumerate(M_BANKS[m]):
                    for k in range(KD):
                        last = pe.matmul(ps_hidden[m][:, c * CAP:(c + 1) * CAP], w1_sb[i][:, k, f * P:(f + 1) * P],
                                         xdT[i][:, k], start=(k == 0), stop=(k == KD - 1))
                last.then_inc(hidden_ready, 1)

            def second_product(e, i, first):
                pe.wait_ge(w2_in[i], loaded(e, i))
                if not first:
                    pe.wait_ge(yT_taken, e)
                for d in range(KD):
                    for k in range(KF):
                        if d == 0 and k in (0, 3, 6):
                            pe.wait_ge(gelu_done, 3 * e + k // 3 + 1)
                        last = pe.matmul(ps_y[:, d * CAP:(d + 1) * CAP], w2_sb[i][:, k, d * P:(d + 1) * P],
                                         hidden[:, k], start=(k == 0), stop=(k == KF - 1))
                last.then_inc(y_ready, 1)

            def yrows_of(e, first):
                pe.wait_ge(yT_taken, e + 1)
                if not first:
                    pe.wait_ge(yrows_taken, e)
                for s in range(2):
                    for d in range(KD):
                        last = pe.transpose(ps_rows[0:SR, s * D + d * P:s * D + (d + 1) * P],
                                            yT[:, d, s * SR:(s + 1) * SR], ident[:])
                last.then_inc(yrows_ready, 1)

            def expert(e, i, before_it, after_it, first, second):
                first_product(e, i, 0, first)
                if before_it:
                    yrows_of(e - 1, second)
                first_product(e, i, 1, first)
                if after_it:
                    xdT_of(e + 1, 1 - i, False)
                first_product(e, i, 2, first)
                second_product(e, i, first)

            pe.wait_ge(scores_taken, B * UNITS)
            pe.wait_ge(att_taken, B * CHUNKS)
            for i in range(2):
                pe.wait_ge(probsT_taken[i], B * UNITS // 2)
            xdT_of(0, 0, True)
            expert(0, 0, False, True, True, False)
            expert(1, 1, True, True, False, True)
            with pe.Fori(1, E // 2 - 1) as turn:
                expert(2 * turn, 0, True, True, False, False)
                expert(2 * turn + 1, 1, True, True, False, False)
            expert(E - 2, 0, True, True, False, False)
            expert(E - 1, 1, True, False, False, False)
            yrows_of(E - 1, False)


_INS = ['x', 'ctx_1024', 'mask_BxS2_bf1', 'g_xattn', 'g_ffn', 'L0_xattn_W_q', 'L0_xattn_b_q', 'L0_xattn_W_k',
        'L0_xattn_b_k', 'L0_xattn_W_v', 'L0_xattn_b_v', 'L0_xattn_W_o', 'L0_xattn_b_o', 'L0_ffn_gate_w',
        'L0_ffn_w1', 'L0_ffn_w2']
_OUTS = [((4, 512, 256), 'float32')]


def kernel(**inputs):
    import numpy as _np
    import concourse.bacc as _bacc
    from concourse import mybir as _mybir
    from concourse.bass_utils import run_bass_kernel_spmd as _run

    nc = _bacc.Bacc("TRN2", target_bir_lowering=False, num_devices=1)
    arrays, args = {}, []
    for name in _INS:
        a = _np.ascontiguousarray(inputs[name])
        if a.dtype.kind == "b":
            a = a.view(_np.uint8)
        arrays[f"in_{name}_dram"] = a
        args.append(nc.dram_tensor(f"in_{name}_dram", a.shape, _mybir.dt.from_np(a.dtype), kind="ExternalInput").ap())
    for i, (shape, dtype) in enumerate(_OUTS):
        dt = _mybir.dt.from_np(_np.dtype(dtype))
        args.append(nc.dram_tensor(f"out_{i}_dram", shape, dt, kind="ExternalOutput").ap())
    flamingo_kernel(nc, *args)
    r = _run(nc, [arrays], core_ids=[0])
    got = tuple(r.results[0][f"out_{i}_dram"] for i in range(len(_OUTS)))
    return got[0]
```

```python
from contextlib import ExitStack

import concourse.bass as bass
from concourse import mybir

F32 = mybir.dt.float32
BF16 = mybir.dt.bfloat16
U32 = mybir.dt.uint32
ALU = mybir.AluOpType
ACT = mybir.ActivationFunctionType
AX = mybir.AxisListType

P = 128
WINDOW = 64
HEADS = 16
EPS = 1e-5
MASKED = 1e30
DROPPED = 8192.0
NO_TOKEN = 1048576.0


def capacity(tokens, experts):
    cap = int(1.25 * tokens // experts)
    return max(cap + cap % 2, 4)


def flamingo_kernel(nc, x, ctx_in, mask, g_xattn, g_ffn, W_q, b_q, W_k, b_k, W_v, b_v, W_o, b_o,
                    gate_w, w1, w2, out):
    B, S, D = x.shape
    E, _, F = w1.shape
    T = S // P
    KD = D // P
    KF = F // P
    NW = S // WINDOW
    HD = D // HEADS
    HG = P // HD
    PAIRS = HG // 2
    CAP = capacity(B * S, E)
    SR = CAP // 2
    ROW = 2 * D + 2
    UNITS = 2 * KD * 4
    CHUNKS = UNITS // 4
    assert (T, KD, NW, HG, UNITS) == (4, 2, 8, 8, 16) and CAP % 32 == 0 and E % 2 == 0

    out_rows = out.rearrange("b s d -> (b s) d")
    queue = nc.dram_tensor("expert_queue", (E * CAP, ROW), F32, kind="Internal").ap()

    es = ExitStack()
    with es:
        def sb(name, shape, dt=F32):
            return es.enter_context(nc.sbuf_tensor(name, shape, dt))

        def sem(name):
            return es.enter_context(nc.semaphore(name))

        ident = sb("ident", [P, P])
        head_mask = sb("head_mask", [P, HG])
        parity_mask = sb("parity_mask", [P, 2])
        causal = sb("causal", [P, 2 * WINDOW], BF16)
        before = sb("before", [P, P], BF16)
        ones = sb("ones", [P, P], BF16)
        countdown = sb("countdown", [P, T, E])
        token_no = sb("token_no", [P, B * T])
        minus_half = sb("minus_half", [P, T])
        eps = sb("eps", [P, T])
        empty_row = sb("empty_row", [P, ROW])
        gates = sb("gates", [P, 2])
        tanh_g = sb("tanh_g", [P, 2])
        bias_qk_raw = sb("bias_qk_raw", [P, 2, KD])
        bias_q = sb("bias_q", [P, KD])
        bias_v = sb("bias_v", [P, D])
        bias_o = sb("bias_o", [P, D])
        bias_og = sb("bias_og", [P, D])
        mask_u8 = sb("mask_u8", [P, B, S], mask.dtype)
        key_valid = sb("key_valid", [P, WINDOW + S], BF16)
        mask_next = sb("mask_next", [P, 2, NW // 2, 2 * WINDOW], BF16)
        mask_now = sb("mask_now", [P, 2, NW // 2, 2 * WINDOW], BF16)
        w_raw = sb("w_raw", [P, 4, KD, D])
        gate_raw = sb("gate_raw", [E, D])
        wT = sb("wT", [P, 4, KD, D])
        gateT = sb("gateT", [P, KD, E])
        x_all = sb("x_all", [P, B, T, D])
        ctx_rows = sb("ctx_rows", [P, T, D])
        xn = sb("xn", [P, T, D])
        stats = sb("stats", [P, B, T, 6])
        mean_var = sb("mean_var", [P, B, T, 2])
        var_eps = sb("var_eps", [P, B, T])
        rstd = sb("rstd", [P, B, T])
        xnT = sb("xnT", [P, KD, S])
        ctxT = sb("ctxT", [P, KD, S])
        qT = sb("qT", [P, KD, S])
        kT = sb("kT", [P, KD, WINDOW + S])
        q_heads = sb("q_heads", [P, KD, NW, HG, WINDOW])
        v = sb("v", [P, T, D])
        v_shift = sb("v_shift", [P, T, D])
        NP_ = 4
        probs = sb("probs", [P, NP_, PAIRS, 2 * WINDOW])
        low = sb("low", [P, NP_, PAIRS])
        total = sb("total", [P, NP_, PAIRS])
        r_total = sb("r_total", [P, NP_, PAIRS])
        NT = 4
        probsT = sb("probsT", [P, NT, PAIRS, 2 * WINDOW])
        attT = sb("attT", [P, KD, S])
        rows = sb("rows", [P, T, ROW])
        stats2 = sb("stats2", [P, T, 6])
        mean_var2 = sb("mean_var2", [P, T, 2])
        var_eps2 = sb("var_eps2", [P, T])
        rstd2 = sb("rstd2", [P, T])
        x1nT = sb("x1nT", [P, KD, S])
        top = sb("top", [P, T])
        lowered = sb("lowered", [P, T, E])
        exps = sb("exps", [P, T, E])
        marks = sb("marks", [P, T, E])
        best = sb("best", [P, T])
        onehot = sb("onehot", [P, T, E], BF16)
        seen = sb("seen", [P, E], BF16)
        seen_add = sb("seen_add", [P, E])
        expsum = sb("expsum", [P, T])
        r_expsum = sb("r_expsum", [P, T])
        ranks = sb("ranks", [P, T, E])
        rank = sb("rank", [P, T])
        past = sb("past", [P, T])
        slot_f = sb("slot_f", [P, T])
        slot = sb("slot", [P, T], U32)
        w1_sb = [sb(f"w1_{i}", [P, KD, F]) for i in range(2)]
        w2_sb = [sb(f"w2_{i}", [P, KF, D]) for i in range(2)]
        q_rows = [sb(f"q_rows{i}", [SR, 2, ROW]) for i in range(2)]
        xdT = [sb(f"xdT{i}", [P, KD, CAP]) for i in range(2)]
        hidden = w_raw[:].rearrange("p w k d -> p (w k d)")[:, 0:KF * CAP].rearrange("p (k c) -> p k c", c=CAP)
        yT = sb("yT", [P, KD, CAP])
        weight = [sb(f"weight{i}", [SR, 2]) for i in range(2)]
        place = [sb(f"place{i}", [SR, 2], U32) for i in range(2)]
        resid = [sb(f"resid{i}", [SR, 2, D]) for i in range(2)]
        y_rows = [sb(f"y_rows{i}", [SR, 2, D]) for i in range(2)]

        bank = [es.enter_context(nc.psum_tensor(f"bank{i}", [P, 512], F32)) for i in range(8)]
        ps_scores, ps_probsT, ps_att, ps_misc = bank[0:2], bank[2:4], bank[4:6], bank[6:8]
        ps_hidden, ps_y, ps_xdT, ps_rows = bank[0:3], bank[3], bank[4], bank[5]

        pool_waited, dve_waited = sem("pool_waited"), sem("dve_waited")
        x_in = [sem(f"x_in{n}") for n in range(B)]
        x_in_late = sem("x_in_late")
        ctx_in_s, small_in, bias_in, mask_in = sem("ctx_in"), sem("small_in"), sem("bias_in"), sem("mask_in")
        w_in = [sem(f"w_in_{w}") for w in "qkvog"]
        v_shifted = [sem("v_shifted_early"), sem("v_shifted_late")]
        prefilled, x1_out = sem("prefilled"), sem("x1_out")
        scattered = sem("scattered")
        w1_in = [sem(f"w1_in{i}") for i in range(2)]
        w2_in = [sem(f"w2_in{i}") for i in range(2)]
        rows_in = [sem(f"rows_in{i}") for i in range(2)]
        y_out = [sem(f"y_out{i}") for i in range(2)]
        const_step, consts_ready, empty_ready = sem("const_step"), sem("consts_ready"), sem("empty_ready")
        mask_step, mask_ready, mask_set = sem("mask_step"), sem("mask_ready"), sem("mask_set")
        tanh_ready, bias_ready = sem("tanh_ready"), sem("bias_ready")
        pads_ready = sem("pads_ready")
        wT_ready, wT_taken = sem("wT_ready"), [sem(f"wT_taken_{w}") for w in "qkvog"]
        x_stat, x_meanvar, x_eps, x_rstd = sem("x_stat"), sem("x_meanvar"), sem("x_eps"), sem("x_rstd")
        xn_ready, x_based = sem("xn_ready"), sem("x_based")
        xnT_ready, xnT_taken = sem("xnT_ready"), sem("xnT_taken")
        ctxT_ready, ctxT_taken = sem("ctxT_ready"), sem("ctxT_taken")
        q_ready, q_taken, q_split = sem("q_ready"), sem("q_taken"), sem("q_split")
        k_ready, k_taken = sem("k_ready"), sem("k_taken")
        v_ready, v_taken = sem("v_ready"), sem("v_taken")
        scores_ready, scores_taken = sem("scores_ready"), sem("scores_taken")
        exp_done, r_total_ready, probs_ready = sem("exp_done"), sem("r_total_ready"), sem("probs_ready")
        probsT_ready = sem("probsT_ready")
        probsT_taken = [sem("probsT_taken_dve"), sem("probsT_taken_act")]
        att_ready, att_even, att_taken = sem("att_ready"), sem("att_even"), sem("att_taken")
        o_ready, x1_ready = sem("o_ready"), sem("x1_ready")
        x1_stat, x1_meanvar, x1_eps, x1_rstd = sem("x1_stat"), sem("x1_meanvar"), sem("x1_eps"), sem("x1_rstd")
        x1n_ready = sem("x1n_ready")
        x1nT_ready, x1nT_taken = sem("x1nT_ready"), sem("x1nT_taken")
        logits_ready, logits_taken, exps_ready = sem("logits_ready"), sem("logits_taken"), sem("exps_ready")
        router_step, onehot_ready, weights_ready = sem("router_step"), sem("onehot_ready"), sem("weights_ready")
        counts_ready, counts_taken, slots_ready = sem("counts_ready"), sem("counts_taken"), sem("slots_ready")
        xdT_ready, xdT_taken, meta_taken = sem("xdT_ready"), sem("xdT_taken"), sem("meta_taken")
        hidden_ready, gelu_done = sem("hidden_ready"), sem("gelu_done")
        y_ready, yT_taken = sem("y_ready"), sem("yT_taken")
        yrows_ready, yrows_taken = sem("yrows_ready"), sem("yrows_taken")

        def value(n, per, k):
            return n * per + k

        def unit(i):
            half, g, wi = i // 8, i // 4 % 2, i % 4
            return half, g, wi, half * 4 + wi

        M_BANKS = [range(0, 3), range(3, 6), range(6, 8)]
        PT_LAG, AV_LAG = 3, 5
        PE_AT = dict(k1=1.5, xnT0=2.0, xnT1=3.0, q0=5.0, q1=5.0, project0=6.0, project1=7.5, ctxT0=8.0, v1=8.0,
                     ctxT1=9.5, x1nT0=10.5, x1nT1=11.5, k0=13.0, route=13.0, count=14.5, v0=15.0)
        ACT_AT = dict(k1=2.0, xnT0=3.0, xnT1=3.0, q0=6.0, q1=7.0, ctxT0=9.0, ctxT1=10.0, x1nT0=10.5, x1nT1=12.0,
                      k0=14.0, exp_logits=15.0)
        DVE_AT = dict(v0=0.5, x_norm=0.5, att2=1.5, split6=2.5, split7=3.5, mask=4.5, att3=5.5, x1_0=6.5, x1_1=7.5,
                      split0=7.5, split1=8.5, att0=10.5, v1=9.5, x1_norm=9.5, split2=10.5, split3=11.5, split4=12.5,
                      att1=13.5, choose=13.5, split5=14.5, rank=15.5)
        STATS_STEPS = (6, 9)
        RANK_STEPS = 5

        rows_last = q_heads[:].rearrange("p k w h q -> p (k w h q)")[:, 0:T * ROW].rearrange("p (t c) -> p t c", c=ROW)

        def rows_of(n):
            return rows_last if isinstance(n, int) and n == B - 1 else rows

        def x1nT_bank(n, m):
            return ps_scores[m] if isinstance(n, int) and n == B - 1 else ps_misc[1 - m]

        def logits_bank(n):
            return ps_probsT[0] if isinstance(n, int) and n == B - 1 else ps_misc[1]

        block = es.enter_context(nc.Block())

        @block.sync
        def _(sp):
            def load_ctx(n):
                if not isinstance(n, int) or n > 0:
                    sp.wait_ge(ctxT_ready, value(n - 1, 2, 2))
                sp.dma_start(ctx_rows[:], ctx_in[n].rearrange("(t p) d -> p t d", p=P)).then_inc(ctx_in_s, 16)

            def shift_v(n, m):
                sp.wait_ge(v_taken, value(n, 2, m + 1))
                first, t0, t1 = max(2 * m, 1), 2 * m, 2 * m + 2
                sp.dma_start(v_shift[WINDOW:P, t0:t1, :], v[0:WINDOW, t0:t1, :]).then_inc(v_shifted[m], 16)
                sp.dma_start(v_shift[0:WINDOW, first:t1, :], v[WINDOW:P, first - 1:t1 - 1, :]).then_inc(v_shifted[m], 16)

            def store_x1(n):
                sp.wait_ge(x1_ready, value(n, 2, 2))
                sp.dma_start(out[n].rearrange("(t p) d -> p t d", p=P), rows_of(n)[:, :, D:2 * D]).then_inc(x1_out, 16)

            def load_w1(e, i):
                sp.dma_start(w1_sb[i][:], w1[e].rearrange("(k p) f -> p k f", p=P)).then_inc(w1_in[i], 16)

            def load_w2(e, i):
                sp.dma_start(w2_sb[i][:], w2[e].rearrange("(k p) d -> p k d", p=P)).then_inc(w2_in[i], 16)

            def load_rows(e, i):
                sp.dma_start(q_rows[i][:], queue[bass.ts(e, CAP), :].rearrange("(s p) c -> p s c", p=SR)
                             ).then_inc(rows_in[i], 16)

            def load_w(i, w):
                sp.dma_start(w_raw[:, i], w.rearrange("(t p) d -> p t d", p=P)).then_inc(w_in[i], 16)

            def load_x(n, t0, t1, loaded_sem):
                sp.dma_start(x_all[:, n, t0:t1], x[n].rearrange("(t p) d -> p t d", p=P)[:, t0:t1]
                             ).then_inc(loaded_sem, 16)

            load_x(0, 0, T // 2, x_in[0])
            load_x(0, T // 2, T, x_in_late)
            load_w(0, W_q)
            load_w(1, W_k)
            load_ctx(0)
            load_w(2, W_v)
            load_x(1, 0, T, x_in[1])
            sp.dma_start(mask_u8[:], mask.partition_broadcast(P)).then_inc(mask_in, 16)
            load_w(3, W_o)
            sp.dma_start(gate_raw[:], gate_w).then_inc(w_in[4], 16)
            for n in range(2, B):
                load_x(n, 0, T, x_in[n])
            sp.wait_ge(empty_ready, 2)
            sp.dma_start(queue.rearrange("(s p) c -> p s c", p=P),
                         empty_row[:].unsqueeze(1).to_broadcast([P, E * CAP // P, ROW])).then_inc(prefilled, 16)

            def body(b, first, last):
                if not last:
                    load_ctx(b + 1)
                shift_v(b, 0)
                shift_v(b, 1)
                if not first:
                    store_x1(b - 1)

            body(0, True, False)
            for e in range(2):
                load_w1(e, e)
                load_w2(e, e)
            with sp.Fori(1, B - 1) as b:
                body(b, False, False)
            body(B - 1, False, True)
            store_x1(B - 1)

            sp.wait_ge(scattered, 16 * T * B)
            for e in range(2):
                load_rows(e, e)

            def reload(e, i):
                sp.wait_ge(xdT_ready, e + 1)
                sp.wait_ge(meta_taken, e + 1)
                load_rows(e + 2, i)
                sp.wait_ge(hidden_ready, 3 * e + 3)
                load_w1(e + 2, i)
                sp.wait_ge(y_ready, e + 1)
                load_w2(e + 2, i)

            with sp.Fori(0, E // 2 - 1) as turn:
                reload(2 * turn, 0)
                reload(2 * turn + 1, 1)

        @block.gpsimd
        def _(pool):
            pool.memset(ident[:], 0.0)
            pool.memset(causal[:], 1.0)
            pool.memset(before[:], 1.0)
            pool.memset(head_mask[:], 1.0)
            pool.memset(parity_mask[:], 0.0)
            pool.memset(ones[:], 1.0)
            pool.memset(minus_half[:], -0.5)
            pool.memset(eps[:], EPS)
            pool.memset(seen[:], 0.0)
            pool.memset(empty_row[:, 0:ROW - 1], 0.0).then_inc(empty_ready, 1)
            pool.memset(empty_row[:, ROW - 1:ROW], NO_TOKEN).then_inc(empty_ready, 1)
            pool.memset(kT[:, :, 0:WINDOW], 0.0).then_inc(pads_ready, 1)
            pool.memset(v_shift[0:WINDOW, 0:1, :], 0.0).then_inc(pads_ready, 1)
            pool.memset(key_valid[:, 0:WINDOW], 0.0).then_inc(const_step, 1)
            pool.wait_ge(const_step, 1)
            pool.affine_select(out=ident[:], in_=ident[:], compare_op=ALU.not_equal, fill=1.0, base=0,
                               pattern=[[-1, P]], channel_multiplier=1)
            pool.affine_select(out=before[:], in_=before[:], compare_op=ALU.is_ge, fill=0.0, base=-1,
                               pattern=[[1, P]], channel_multiplier=-1).then_inc(const_step, 1)
            for h in range(2):
                q = slice(h * WINDOW, (h + 1) * WINDOW)
                pool.wait_ge(const_step, 2 + h)
                pool.affine_select(out=causal[q, WINDOW:], in_=causal[q, WINDOW:], compare_op=ALU.is_ge, fill=0.0,
                                   base=0, pattern=[[-1, WINDOW]], channel_multiplier=1).then_inc(const_step, 1)
            pool.wait_ge(const_step, 4)
            pool.affine_select(out=head_mask[:], in_=head_mask[:], compare_op=ALU.is_ge, fill=0.0, base=0,
                               pattern=[[-HD, HG]], channel_multiplier=1).then_inc(const_step, 1)
            pool.wait_ge(const_step, 5)
            pool.affine_select(out=head_mask[:], in_=head_mask[:], compare_op=ALU.is_ge, fill=0.0, base=HD - 1,
                               pattern=[[HD, HG]], channel_multiplier=-1).then_inc(const_step, 1)
            pool.iota(countdown[:], pattern=[[0, T], [-1, E]], base=E, channel_multiplier=0,
                      allow_small_or_imprecise_dtypes=True)
            pool.iota(token_no[:], pattern=[[P, B * T]], base=0, channel_multiplier=1,
                      allow_small_or_imprecise_dtypes=True).then_inc(consts_ready, 1)
            def x_rstd_of(n):
                pool.wait_ge(x_meanvar, value(n, 1, 1))
                pool.tensor_tensor(var_eps[:, n], mean_var[:, n, :, 1], eps[:], ALU.add).then_inc(x_eps, 1)
                pool.wait_ge(x_eps, value(n, 1, 1))
                pool.tensor_tensor(rstd[:, n], var_eps[:, n], minus_half[:], ALU.pow).then_inc(x_rstd, 1)

            x_rstd_of(0)
            pool.wait_ge(const_step, 6)
            for h in range(HG):
                pool.tensor_tensor(parity_mask[:, h % 2:h % 2 + 1], parity_mask[:, h % 2:h % 2 + 1],
                                   head_mask[:, h:h + 1], ALU.add).then_inc(const_step, 1)
                pool.wait_ge(const_step, 7 + h)

            def base_of(n):
                pool.wait_ge(xn_ready, value(n, 1, 1))
                pool.wait_ge(bias_ready, 2)
                pool.tensor_tensor(x_all[:, n], x_all[:, n], bias_og[:].unsqueeze(1).to_broadcast([P, T, D]),
                                   ALU.add).then_inc(x_based, 1)

            def norm(n, i):
                pool.wait_ge(r_total_ready, value(n, UNITS, i + 1))
                pool.tensor_tensor(probs[:, i % NP_], probs[:, i % NP_],
                                   r_total[:, i % NP_].unsqueeze(2).to_broadcast([P, PAIRS, 2 * WINDOW]),
                                   ALU.mult).then_inc(probs_ready, 1)

            def x1_rstd_of(n, m):
                tiles = slice(2 * m, 2 * m + 2)
                pool.wait_ge(x1_meanvar, value(n, 2, m + 1))
                pool.tensor_tensor(var_eps2[:, tiles], mean_var2[:, tiles, 1], eps[:, tiles], ALU.add).then_inc(x1_eps, 1)
                pool.wait_ge(x1_eps, value(n, 2, m + 1))
                pool.tensor_tensor(rstd2[:, tiles], var_eps2[:, tiles], minus_half[:, tiles], ALU.pow
                                   ).then_inc(x1_rstd, 1)

            def scatter(n):
                pool.wait_ge(prefilled, 16)
                pool.wait_ge(slots_ready, value(n, 1, 1))
                pool.wait_ge(weights_ready, value(n, 2, 2))
                pool.wait_ge(x1n_ready, value(n, 2, 2))
                pool.sem_inc(pool_waited, 1)
                for t in range(T):
                    pool.indirect_dma_start(out=queue, out_offset=bass.IndirectOffsetOnAxis(ap=slot[:, t:t + 1], axis=0),
                                            in_=rows_of(n)[:, t, :], in_offset=None, bounds_check=E * CAP - 1,
                                            oob_is_err=False).then_inc(scattered, 16)

            def body(b, first, last):
                for i in range(UNITS + (1 if last else 0)):
                    if i > 0 or not first:
                        norm(b, i - 1)
                    if first and i in STATS_STEPS:
                        x_rstd_of(2 + STATS_STEPS.index(i))
                    if i == 3 and not last:
                        base_of(b + 1)
                    if i == 8 and not first:
                        x1_rstd_of(b - 1, 0)
                        x1_rstd_of(b - 1, 1)
                    if i == (UNITS if last else 15) and not first:
                        scatter(b - 1)

            x_rstd_of(1)
            base_of(0)
            body(0, True, False)
            with pool.Fori(1, B - 1) as b:
                body(b, False, False)
            body(B - 1, False, True)
            x1_rstd_of(B - 1, 0)
            x1_rstd_of(B - 1, 1)
            scatter(B - 1)

            def place_rows(e, i):
                pool.wait_ge(x1_out, 16 * B)
                pool.wait_ge(yrows_taken, e + 1)
                pool.sem_inc(pool_waited, 1)
                for s in range(2):
                    pool.indirect_dma_start(out=out_rows,
                                            out_offset=bass.IndirectOffsetOnAxis(ap=place[i][:, s:s + 1], axis=0),
                                            in_=y_rows[i][:, s, :], in_offset=None, bounds_check=B * S - 1,
                                            oob_is_err=False).then_inc(y_out[i], 16)

            with pool.Fori(0, E // 2) as turn:
                place_rows(2 * turn, 0)
                place_rows(2 * turn + 1, 1)
            for i in range(2):
                pool.wait_ge(y_out[i], 16 * E)

        @block.scalar
        def _(act):
            for i, b in enumerate((b_q, b_k)):
                act.dma_start(bias_qk_raw[:, i], b.rearrange("(g p) -> p g", p=P),
                              allow_slow_non_contiguous=True).then_inc(bias_in, 16)
            act.dma_start(gates[:, 0:1], g_xattn.partition_broadcast(P)).then_inc(small_in, 16)
            act.dma_start(gates[:, 1:2], g_ffn.partition_broadcast(P)).then_inc(small_in, 16)
            act.dma_start(bias_v[:], b_v.partition_broadcast(P)).then_inc(small_in, 16)
            act.dma_start(bias_o[:], b_o.partition_broadcast(P)).then_inc(small_in, 16)

            def take_wT(i, step):
                act.wait_ge(wT_ready, step)
                act.activation(wT[:, i], bank[i][:].rearrange("p (k d) -> p k d", k=KD), ACT.Copy).then_inc(wT_taken[i], 1)

            def take_xnT(n, k):
                act.wait_ge(xnT_ready, value(n, 2, k + 1))
                act.activation(xnT[:, k], ps_misc[k][:], ACT.Copy).then_inc(xnT_taken, 1)

            def take_q(n, g):
                act.wait_ge(q_ready, value(n, 2, g + 1))
                if not isinstance(n, int) or n > 0:
                    act.wait_ge(q_split, value(n - 1, 2 * CHUNKS, 2 * CHUNKS))
                act.activation(qT[:, g], ps_misc[g][:], ACT.Identity, bias=bias_q[:, g:g + 1],
                               scale=-float(HD) ** -0.5).then_inc(q_taken, 1)

            def take_ctxT(n, k):
                act.wait_ge(ctxT_ready, value(n, 2, k + 1))
                act.wait_ge(v_ready, value(n - 1, 2, 2))
                act.activation(ctxT[:, k], ps_misc[0][:], ACT.Copy).then_inc(ctxT_taken, 1)

            def take_k(n, g):
                act.wait_ge(k_ready, value(n, 2, g + 1))
                if not isinstance(n, int) or n > 0:
                    act.wait_ge(scores_ready, value(n - 1, UNITS, UNITS - 4 + 4 * g))
                act.activation(kT[:, g, WINDOW:], ps_misc[g][:], ACT.Identity,
                               bias=bias_qk_raw[:, 1, g:g + 1]).then_inc(k_taken, 1)

            def exp(n, i):
                act.wait_ge(scores_taken, value(n, UNITS, i + 1))
                for j in range(PAIRS):
                    last = act.activation(probs[:, i % NP_, j], probs[:, i % NP_, j], ACT.Exp, scale=-1.0,
                                          bias=low[:, i % NP_, j:j + 1], accum_out=total[:, i % NP_, j:j + 1])
                last.then_inc(exp_done, 1)

            def take_probsT(n, i):
                act.wait_ge(probsT_ready, value(n, UNITS, i + 1))
                if i >= NT or not isinstance(n, int) or n > 0:
                    act.wait_ge(att_ready, value(n, UNITS, i - NT + 1))
                act.activation(probsT[:, i % NT], ps_probsT[i % 2][:].rearrange("p (j q) -> p j q", j=PAIRS),
                               ACT.Copy).then_inc(probsT_taken[1], 1)

            def take_x1nT(n, m):
                act.wait_ge(x1nT_ready, value(n, 2, m + 1))
                act.activation(x1nT[:, :, 2 * m * P:(2 * m + 2) * P], x1nT_bank(n, m)[:].rearrange("p (k t) -> p k t", k=KD),
                               ACT.Copy).then_inc(x1nT_taken, 1)

            def exp_logits(n):
                act.wait_ge(logits_taken, value(n, 1, 1))
                act.activation(exps[:], lowered[:], ACT.Exp).then_inc(exps_ready, 1)

            def rest(at, b, first, last):
                if first and at == 1.5:
                    take_wT(3, 4)
                if at == ACT_AT["k1"]:
                    take_k(b, 1)
                if not last:
                    for k in range(2):
                        if at == ACT_AT[f"xnT{k}"]:
                            take_xnT(b + 1, k)
                    for k in range(2):
                        if at == ACT_AT[f"q{k}"]:
                            take_q(b + 1, k)
                    for k in range(2):
                        if at == ACT_AT[f"ctxT{k}"]:
                            take_ctxT(b + 1, k)
                if not first:
                    for m in range(2):
                        if at == ACT_AT[f"x1nT{m}"]:
                            take_x1nT(b - 1, m)
                if not last and at == ACT_AT["k0"]:
                    take_k(b + 1, 0)
                if not first and at == ACT_AT["exp_logits"]:
                    exp_logits(b - 1)

            def body(b, first, last):
                for i in range(UNITS + (PT_LAG if last else 0)):
                    rest(i, b, first, last)
                    if i < UNITS:
                        exp(b, i)
                    if (i >= PT_LAG or not first) and (i - PT_LAG) % 2 == 1:
                        take_probsT(b, i - PT_LAG)
                    rest(i + 0.5, b, first, last)

            take_wT(0, 1)
            take_wT(1, 2)
            for k in range(KD):
                take_xnT(0, k)
            act.wait_ge(bias_in, 2 * 16)
            act.wait_ge(bias_ready, 1)
            take_q(0, 0)
            take_k(0, 0)
            take_q(0, 1)
            take_wT(2, 3)
            act.wait_ge(small_in, 4 * 16)
            act.activation(tanh_g[:], gates[:], ACT.Tanh).then_inc(tanh_ready, 1)
            body(0, True, False)
            with act.Fori(1, B - 1) as b:
                body(b, False, False)
            body(B - 1, False, True)
            for k in range(KD):
                take_x1nT(B - 1, k)
            exp_logits(B - 1)

            def gelu(e, first):
                for m, ms in enumerate(M_BANKS):
                    act.wait_ge(hidden_ready, 3 * e + m + 1)
                    if not first:
                        act.wait_ge(y_ready, e)
                    n = len(ms) * CAP
                    act.activation(hidden[:, ms[0]:ms[-1] + 1, :], ps_hidden[m][:, 0:n].rearrange("p (m c) -> p m c", c=CAP),
                                   ACT.Gelu_apprx_tanh).then_inc(gelu_done, 1)

            gelu(0, True)
            gelu(1, False)
            with act.Fori(1, E // 2) as turn:
                gelu(2 * turn, False)
                gelu(2 * turn + 1, False)

        @block.vector
        def _(dve):
            def x_stats(n):
                dve.wait_ge(x_in[n], 16)
                for t in range(T):
                    if n == 0 and t == T // 2:
                        dve.wait_ge(x_in_late, 16)
                    last = dve.bn_stats(stats[:, n, t], x_all[:, n, t])
                last.then_inc(x_stat, 1)
                dve.wait_ge(x_stat, n + 1)
                for t in range(T):
                    last = dve.bn_aggr(mean_var[:, n, t], stats[:, n, t])
                last.then_inc(x_meanvar, 1)

            def x_norm(n):
                dve.wait_ge(x_rstd, value(n, 1, 1))
                if not isinstance(n, int) or n > 0:
                    dve.wait_ge(xnT_ready, value(n - 1, 2, 2))
                for t in range(T):
                    last = dve.tensor_scalar(xn[:, t], x_all[:, n, t], mean_var[:, n, t, 0:1], rstd[:, n, t:t + 1],
                                             ALU.subtract, ALU.mult)
                last.then_inc(xn_ready, 1)

            def mask_of(n):
                if not isinstance(n, int) or n > 0:
                    dve.wait_ge(mask_set, value(n, 1, 0))
                dve.tensor_copy(key_valid[:, WINDOW:], mask_u8[:, n]).then_inc(mask_step, 1)
                dve.wait_ge(mask_step, value(n, 1, 1))
                for e in range(2):
                    keys = key_valid[:, e * WINDOW:e * WINDOW + S].rearrange("p (w k) -> p w k", k=2 * WINDOW)
                    dve.tensor_tensor(mask_next[:, e], keys,
                                      causal[:].unsqueeze(1).to_broadcast([P, NW // 2, 2 * WINDOW]),
                                      ALU.mult).then_inc(mask_ready, 1)

            def take_v(n, m):
                dve.wait_ge(v_ready, value(n, 2, m + 1))
                if not isinstance(n, int) or n > 0:
                    dve.wait_ge(att_ready, value(n - 1, UNITS, UNITS // 2 * (m + 1)))
                    for part in v_shifted:
                        dve.wait_ge(part, 32 * n)
                dve.tensor_tensor(v[:, 2 * m:2 * m + 2], ps_misc[m][:].rearrange("p (t d) -> p t d", d=D),
                                  bias_v[:].unsqueeze(1).to_broadcast([P, 2, D]), ALU.add).then_inc(v_taken, 1)

            def low_of(n, i):
                _, _, _, w = unit(i)
                dve.wait_ge(scores_ready, value(n, UNITS, i + 1))
                if i >= NP_:
                    dve.wait_ge(probsT_ready, value(n, UNITS, i - NP_ + 1))
                elif not isinstance(n, int) or n > 0:
                    dve.wait_ge(probsT_ready, value(n - 1, UNITS, UNITS + i - NP_ + 1))
                if i == 0:
                    dve.wait_ge(mask_ready, value(n, 2, 2))
                    if not isinstance(n, int) or n > 0:
                        dve.wait_ge(scores_taken, value(n - 1, UNITS, UNITS))
                    dve.tensor_scalar(mask_now[:], mask_next[:], -MASKED, MASKED, ALU.mult, ALU.add
                                      ).then_inc(mask_set, 1)
                    dve.wait_ge(mask_set, value(n, 1, 1))
                dve.sem_inc(dve_waited, 1)
                for j in range(PAIRS):
                    last = dve.tensor_tensor_reduce(
                        probs[:, i % NP_, j], ps_scores[i % 2][:, j * P:(j + 1) * P], mask_now[:, w % 2, w // 2],
                        1.0, 3.0e38, ALU.add, ALU.min, low[:, i % NP_, j:j + 1])
                last.then_inc(scores_taken, 1)

            def r_total_of(n, i):
                dve.wait_ge(exp_done, value(n, UNITS, i + 1))
                dve.reciprocal(r_total[:, i % NP_], total[:, i % NP_]).then_inc(r_total_ready, 1)

            def take_probsT(n, i):
                dve.wait_ge(probsT_ready, value(n, UNITS, i + 1))
                if i >= NT or not isinstance(n, int) or n > 0:
                    dve.wait_ge(att_ready, value(n, UNITS, i - NT + 1))
                dve.tensor_copy(probsT[:, i % NT], ps_probsT[i % 2][:].rearrange("p (j q) -> p j q", j=PAIRS)
                                ).then_inc(probsT_taken[0], 1)

            def take_att(n, c):
                half, g, _, _ = unit(4 * c)
                dve.wait_ge(att_ready, value(n, UNITS, 4 * c + 4))
                if not isinstance(n, int) or n > 0:
                    dve.wait_ge(o_ready, value(n - 1, 2, half + 1))
                src = ps_att[c % 2][:].rearrange("p (w e q) -> p w e q", w=4, e=2)
                dst = attT[:, g, half * 4 * WINDOW:(half + 1) * 4 * WINDOW].rearrange("p (w q) -> p w q", q=WINDOW)
                dve.tensor_scalar(dst, src[:, :, 0], parity_mask[:, 0:1], None, ALU.mult).then_inc(att_even, 1)
                dve.wait_ge(att_even, value(n, CHUNKS, c + 1))
                dve.scalar_tensor_tensor(dst, src[:, :, 1], parity_mask[:, 1:2], dst, ALU.mult, ALU.add
                                         ).then_inc(att_taken, 1)

            def split_q(n, part):
                c, h0 = part // 2, part % 2 * 4
                half, g, _, _ = unit(4 * c)
                if part % 2 == 0:
                    dve.wait_ge(q_taken, value(n, 2, g + 1))
                    if not isinstance(n, int) or n > 0:
                        dve.wait_ge(scores_ready, value(n - 1, UNITS, 4 * c + 4))
                src = qT[:, g, half * 4 * WINDOW:(half + 1) * 4 * WINDOW].rearrange("p (w q) -> p w q", q=WINDOW)
                for h in range(h0, h0 + 4):
                    last = dve.tensor_scalar(q_heads[:, g, half * 4:half * 4 + 4, h, :], src,
                                              head_mask[:, h:h + 1], None, ALU.mult)
                last.then_inc(q_split, 1)

            def x1_of(n, k):
                dve.wait_ge(o_ready, value(n, 2, k + 1))
                dve.wait_ge(x_based, value(n, 1, 1))
                if isinstance(n, int) and n == B - 1:
                    dve.wait_ge(scores_ready, B * UNITS)
                elif not isinstance(n, int) or n > 0:
                    dve.wait_ge(x1_out, 16 * n)
                    dve.wait_ge(scattered, 16 * T * n)
                dve.scalar_tensor_tensor(rows_of(n)[:, 2 * k:2 * k + 2, D:2 * D],
                                         ps_misc[k][:].rearrange("p (t d) -> p t d", d=D), tanh_g[:, 0:1],
                                         x_all[:, n, 2 * k:2 * k + 2], ALU.mult, ALU.add).then_inc(x1_ready, 1)

            def x1_stats(n, m):
                dve.wait_ge(x1_ready, value(n, 2, m + 1))
                for t in range(2 * m, 2 * m + 2):
                    last = dve.bn_stats(stats2[:, t], rows_of(n)[:, t, D:2 * D])
                last.then_inc(x1_stat, 1)
                dve.wait_ge(x1_stat, value(n, 2, m + 1))
                dve.sem_inc(dve_waited, 1)
                for t in range(2 * m, 2 * m + 2):
                    last = dve.bn_aggr(mean_var2[:, t], stats2[:, t])
                last.then_inc(x1_meanvar, 1)

            def x1_norm(n, m):
                dve.wait_ge(x1_rstd, value(n, 2, m + 1))
                for t in range(2 * m, 2 * m + 2):
                    last = dve.tensor_scalar(rows_of(n)[:, t, 0:D], rows_of(n)[:, t, D:2 * D], mean_var2[:, t, 0:1],
                                             rstd2[:, t:t + 1], ALU.subtract, ALU.mult)
                last.then_inc(x1n_ready, 1)

            def choose(n):
                def done(k):
                    dve.wait_ge(router_step, value(n, RANK_STEPS + 3, k))
                dve.wait_ge(logits_ready, value(n, 1, 1))
                logits = logits_bank(n)[:, 0:T * E].rearrange("p (t e) -> p t e", e=E)
                dve.tensor_reduce(top[:], logits, AX.X, ALU.max).then_inc(router_step, 1)
                done(1)
                dve.tensor_tensor(lowered[:], logits, top[:].unsqueeze(2).to_broadcast([P, T, E]), ALU.subtract
                                  ).then_inc(logits_taken, 1)
                dve.wait_ge(logits_taken, value(n, 1, 1))
                dve.scalar_tensor_tensor(marks[:], lowered[:], 0.0, countdown[:], ALU.is_ge, ALU.mult
                                         ).then_inc(router_step, 1)
                done(2)
                dve.tensor_reduce(best[:], marks[:], AX.X, ALU.max).then_inc(router_step, 1)
                done(3)
                dve.tensor_tensor(onehot[:], marks[:], best[:].unsqueeze(2).to_broadcast([P, T, E]), ALU.is_equal
                                  ).then_inc(onehot_ready, 1)

            def weights_of(n):
                def done(k):
                    dve.wait_ge(router_step, value(n, RANK_STEPS + 3, 3 + k))
                dve.wait_ge(exps_ready, value(n, 1, 1))
                dve.tensor_reduce(expsum[:], exps[:], AX.X, ALU.add).then_inc(router_step, 1)
                done(1)
                dve.reciprocal(r_expsum[:], expsum[:]).then_inc(router_step, 1)
                done(2)
                dve.tensor_scalar(rows_of(n)[:, :, 2 * D], r_expsum[:], tanh_g[:, 1:2], None, ALU.mult
                                  ).then_inc(weights_ready, 1)
                dve.tensor_copy(rows_of(n)[:, :, 2 * D + 1], token_no[:, bass.ts(n, T)]).then_inc(weights_ready, 1)

            def rank_of(n):
                def done(k):
                    dve.wait_ge(router_step, value(n, RANK_STEPS + 3, 3 + k))
                if isinstance(n, int) and n == B - 1:
                    dve.wait_ge(scattered, 16 * T * n)
                dve.wait_ge(counts_ready, value(n, 1, 1))
                counts = ps_misc[1][:, 0:T * E].rearrange("p (t e) -> p t e", e=E)
                dve.tensor_tensor(ranks[:], counts, onehot[:], ALU.mult).then_inc(counts_taken, 1)
                dve.wait_ge(counts_taken, value(n, 1, 1))
                dve.tensor_reduce(rank[:], ranks[:], AX.X, ALU.add).then_inc(router_step, 1)
                dve.tensor_reduce(seen_add[:], onehot[:].rearrange("p t e -> p e t"), AX.X, ALU.add
                                  ).then_inc(router_step, 1)
                done(4)
                dve.tensor_tensor(seen[:], seen[:], seen_add[:], ALU.add)
                dve.tensor_scalar(past[:], rank[:], float(CAP), DROPPED, ALU.is_ge, ALU.mult)
                dve.scalar_tensor_tensor(slot_f[:], best[:], -float(CAP), rank[:], ALU.mult, ALU.add
                                         ).then_inc(router_step, 1)
                done(5)
                dve.scalar_tensor_tensor(slot[:], slot_f[:], float(E * CAP), past[:], ALU.add, ALU.add
                                         ).then_inc(slots_ready, 1)

            def rest(at, b, first, last):
                if first and at == 0.5:
                    dve.wait_ge(small_in, 4 * 16)
                    dve.wait_ge(tanh_ready, 1)
                    dve.tensor_scalar(bias_og[:], bias_o[:], tanh_g[:, 0:1], None, ALU.mult).then_inc(bias_ready, 1)
                if first and at == 2.5:
                    dve.wait_ge(wT_ready, 5)
                    dve.tensor_copy(gateT[:], bank[5][:, 0:KD * E].rearrange("p (k e) -> p k e", e=E)
                                    ).then_inc(wT_taken[4], 1)
                for c in (2, 3):
                    if not first and at == DVE_AT[f"att{c}"]:
                        take_att(b - 1, c)
                for c in (0, 1):
                    if at == DVE_AT[f"att{c}"]:
                        take_att(b, c)
                for c in (2, 3):
                    if last and at == DVE_AT[f"att{c}"] + UNITS:
                        take_att(b, c)
                if at == DVE_AT["v0"]:
                    take_v(b, 0)
                if first and at < 6 and at % 1:
                    split_q(b, 2 + int(at))
                for part in (6, 7):
                    if not first and at == DVE_AT[f"split{part}"]:
                        split_q(b, part)
                for part in range(6):
                    if not last and at == DVE_AT[f"split{part}"]:
                        split_q(b + 1, part)
                if first and at % 1 and int(at) in STATS_STEPS:
                    x_stats(2 + STATS_STEPS.index(int(at)))
                if not last and at == DVE_AT["x_norm"]:
                    x_norm(b + 1)
                if not last and at == DVE_AT["mask"]:
                    mask_of(b + 1)
                for m in range(2):
                    if not first and at == DVE_AT[f"x1_{m}"]:
                        x1_of(b - 1, m)
                        x1_stats(b - 1, m)
                if at == DVE_AT["v1"]:
                    take_v(b, 1)
                if not first and at == DVE_AT["x1_norm"]:
                    x1_norm(b - 1, 0)
                    x1_norm(b - 1, 1)
                if not first and at == DVE_AT["choose"]:
                    choose(b - 1)
                if last and at == UNITS + 1.5:
                    x1_of(b, 0)
                    x1_stats(b, 0)
                if not first and at == DVE_AT["rank"]:
                    weights_of(b - 1)
                    rank_of(b - 1)

            def body(b, first, last):
                for i in range(UNITS + (6 if last else 0)):
                    rest(i, b, first, last)
                    if i < UNITS:
                        low_of(b, i)
                    if (i >= 1 or not first) and i - 1 < UNITS:
                        r_total_of(b, i - 1)
                    rest(i + 0.5, b, first, last)
                    if (i >= PT_LAG or not first) and i - PT_LAG < UNITS and (i - PT_LAG) % 2 == 0:
                        take_probsT(b, i - PT_LAG)

            x_stats(0)
            x_norm(0)
            dve.wait_ge(bias_in, 2 * 16)
            dve.tensor_scalar(bias_q[:], bias_qk_raw[:, 0], -float(HD) ** -0.5, None, ALU.mult).then_inc(bias_ready, 1)
            for k in range(KD):
                dve.wait_ge(ctxT_ready, k + 1)
                dve.tensor_copy(ctxT[:, k], bank[4 + k][:]).then_inc(ctxT_taken, 1)
            dve.wait_ge(mask_in, 16)
            dve.wait_ge(consts_ready, 1)
            mask_of(0)
            x_stats(1)
            for part in range(2):
                split_q(0, part)
            body(0, True, False)
            with dve.Fori(1, B - 1) as b:
                body(b, False, False)
            body(B - 1, False, True)
            x1_norm(B - 1, 0)
            x1_of(B - 1, 1)
            x1_stats(B - 1, 1)
            x1_norm(B - 1, 1)
            choose(B - 1)
            weights_of(B - 1)
            rank_of(B - 1)

            def take_xd(e, i, first):
                dve.wait_ge(xdT_ready, e + 1)
                if not first:
                    dve.wait_ge(hidden_ready, 3 * e - 3)
                    dve.wait_ge(y_out[i], 16 * (e - i))
                dve.tensor_copy(xdT[i][:], ps_xdT[:, 0:KD * CAP].rearrange("p (k c) -> p k c", c=CAP)
                                ).then_inc(xdT_taken, 1)
                dve.tensor_copy(place[i][:], q_rows[i][:, :, 2 * D + 1])
                dve.tensor_copy(weight[i][:], q_rows[i][:, :, 2 * D])
                dve.tensor_copy(resid[i][:], q_rows[i][:, :, D:2 * D]).then_inc(meta_taken, 1)

            def take_yT(e):
                dve.wait_ge(y_ready, e + 1)
                dve.tensor_copy(yT[:], ps_y[:, 0:KD * CAP].rearrange("p (k c) -> p k c", c=CAP)).then_inc(yT_taken, 1)

            def take_yrows(e, i):
                dve.wait_ge(yrows_ready, e + 1)
                dve.wait_ge(meta_taken, e + 1)
                for s in range(2):
                    last = dve.scalar_tensor_tensor(y_rows[i][:, s], ps_rows[0:SR, s * D:(s + 1) * D],
                                                    weight[i][:, s:s + 1], resid[i][:, s], ALU.mult, ALU.add)
                last.then_inc(yrows_taken, 1)

            def expert(e, i, before_it, after_it, first):
                if before_it:
                    take_yrows(e - 1, 1 - i)
                if after_it:
                    take_xd(e + 1, 1 - i, first)
                take_yT(e)

            take_xd(0, 0, True)
            expert(0, 0, False, True, True)
            expert(1, 1, True, True, False)
            with dve.Fori(1, E // 2 - 1) as turn:
                expert(2 * turn, 0, True, True, False)
                expert(2 * turn + 1, 1, True, True, False)
            expert(E - 2, 0, True, True, False)
            expert(E - 1, 1, True, False, False)
            take_yrows(E - 1, 1)

        @block.tensor
        def _(pe):
            def wT_of(i):
                pe.wait_ge(w_in[i], 16)
                for k in range(KD):
                    for d in range(KD):
                        last = pe.transpose(bank[i][:, k * D + d * P:k * D + (d + 1) * P],
                                            w_raw[:, i, d, k * P:(k + 1) * P], ident[:])
                last.then_inc(wT_ready, 1)

            def xnT_of(n, k, free=None, least=0):
                pe.wait_ge(xn_ready, value(n, 1, 1))
                if free is not None:
                    pe.wait_ge(free, least)
                for t in range(T):
                    last = pe.transpose(ps_misc[k][:, t * P:(t + 1) * P], xn[:, t, k * P:(k + 1) * P], ident[:])
                last.then_inc(xnT_ready, 1)

            def ctxT_of(n, k, ps, free=None, least=0):
                pe.wait_ge(ctx_in_s, 16 * (n + 1))
                if free is not None:
                    pe.wait_ge(free, least)
                for t in range(T):
                    last = pe.transpose(ps[:, t * P:(t + 1) * P], ctx_rows[:, t, k * P:(k + 1) * P], ident[:])
                last.then_inc(ctxT_ready, 1)

            def q_of(n, g):
                pe.wait_ge(xnT_taken, value(n, 2, 2))
                for k in range(KD):
                    last = pe.matmul(ps_misc[g][:], wT[:, 0, k, g * P:(g + 1) * P], xnT[:, k], start=(k == 0),
                                     stop=(k == KD - 1))
                last.then_inc(q_ready, 1)

            def k_of(n, g, free, least):
                pe.wait_ge(free, least)
                pe.wait_ge(ctxT_taken, value(n, 2, 2))
                for k in range(KD):
                    last = pe.matmul(ps_misc[g][:], wT[:, 1, k, g * P:(g + 1) * P], ctxT[:, k], start=(k == 0),
                                     stop=(k == KD - 1))
                last.then_inc(k_ready, 1)

            def v_of(n, m, free, least):
                pe.wait_ge(free, least)
                for t in range(2 * m, 2 * m + 2):
                    for k in range(KD):
                        last = pe.matmul(ps_misc[m][:, t % 2 * D:(t % 2 + 1) * D], ctxT[:, k, t * P:(t + 1) * P],
                                         wT[:, 2, k], start=(k == 0), stop=(k == KD - 1))
                last.then_inc(v_ready, 1)

            def scores(n, i):
                _, g, _, w = unit(i)
                if i % 4 == 0:
                    pe.wait_ge(q_split, value(n, 2 * CHUNKS, 2 * (i // 4) + 2))
                if i in (0, 4):
                    pe.wait_ge(k_taken, value(n, 2, 1 + i // 4))
                if i >= 2:
                    pe.wait_ge(scores_taken, value(n, UNITS, i - 1))
                elif not isinstance(n, int) or n > 0:
                    pe.wait_ge(scores_taken, value(n - 1, UNITS, UNITS + i - 1))
                for j in range(PAIRS):
                    last = pe.matmul(ps_scores[i % 2][:, j * P:(j + 1) * P],
                                     q_heads[:, g, w, 2 * j:2 * j + 2, :],
                                     kT[:, g, w * WINDOW:w * WINDOW + 2 * WINDOW], start=True, stop=True)
                last.then_inc(scores_ready, 1)

            def probsT_of(n, i):
                pe.wait_ge(probs_ready, value(n, UNITS, i + 1))
                if i >= 2 or not isinstance(n, int) or n > 0:
                    pe.wait_ge(probsT_taken[i % 2], value(n, UNITS // 2, i // 2))
                for j in range(PAIRS):
                    last = pe.transpose(ps_probsT[i % 2][:, j * P:(j + 1) * P], probs[:, i % NP_, j], ident[:])
                last.then_inc(probsT_ready, 1)

            def attend(n, i):
                _, g, wi, w = unit(i % UNITS)
                c = i // 4
                pe.wait_ge(probsT_taken[i % 2], value(n, UNITS // 2, i // 2 + 1))
                if i in (0, 8):
                    pe.wait_ge(v_taken, value(n, 2, 1 + i // 8))
                    pe.wait_ge(v_shifted[i // 8], 32 * (n + 1))
                if wi == 0 and (c >= 2 or not isinstance(n, int) or n > 0):
                    pe.wait_ge(att_taken, value(n, CHUNKS, c - 1))
                src = v if w % 2 else v_shift
                for j in range(PAIRS):
                    last = pe.matmul(ps_att[c % 2][j * 32:(j + 1) * 32, wi * P:(wi + 1) * P],
                                     src[:, w // 2, g * P + j * 32:g * P + (j + 1) * 32], probsT[:, i % NT, j],
                                     start=True, stop=True)
                last.then_inc(att_ready, 1)

            def project(n, m, free, least):
                pe.wait_ge(free, least)
                pe.wait_ge(att_taken, value(n, CHUNKS, CHUNKS // 2 * (m + 1)))
                for t in range(2 * m, 2 * m + 2):
                    for g in range(KD):
                        last = pe.matmul(ps_misc[m][:, t % 2 * D:(t % 2 + 1) * D], attT[:, g, t * P:(t + 1) * P],
                                         wT[:, 3, g], start=(g == 0), stop=(g == KD - 1))
                last.then_inc(o_ready, 1)

            def x1nT_of(n, m, free, least):
                if free is not None:
                    pe.wait_ge(free, least)
                pe.wait_ge(x1n_ready, value(n, 2, m + 1))
                for k in range(KD):
                    for t in range(2):
                        last = pe.transpose(x1nT_bank(n, m)[:, (2 * k + t) * P:(2 * k + t + 1) * P],
                                            rows_of(n)[:, 2 * m + t, k * P:(k + 1) * P], ident[:])
                last.then_inc(x1nT_ready, 1)

            def route(n):
                for t in range(T):
                    if t % 2 == 0:
                        pe.wait_ge(x1nT_taken, value(n, 2, 1 + t // 2))
                    for k in range(KD):
                        last = pe.matmul(logits_bank(n)[:, t * E:(t + 1) * E], x1nT[:, k, t * P:(t + 1) * P],
                                         gateT[:, k], start=(k == 0), stop=(k == KD - 1))
                last.then_inc(logits_ready, 1)

            def count(n):
                pe.wait_ge(onehot_ready, value(n, 1, 1))
                if not isinstance(n, int) or n > 0:
                    pe.wait_ge(slots_ready, value(n - 1, 1, 1))
                bank_ = ps_misc[1][:, 0:T * E]
                pe.matmul(bank_, ones[:], seen[:].unsqueeze(1).to_broadcast([P, T, E]), start=True, stop=False,
                          skip_group_check=True)
                for t in range(T - 1):
                    pe.matmul(bank_[:, (t + 1) * E:], ones[:],
                              onehot[:, t:t + 1].to_broadcast([P, T - 1 - t, E]), start=False, stop=False,
                              skip_group_check=True)
                pe.matmul(bank_, before[:], onehot[:], start=False, stop=True, skip_group_check=True
                          ).then_inc(counts_ready, 1)

            def rest(at, b, first, last):
                if first and at == 0:
                    pe.wait_ge(wT_taken[2], 1)
                    v_of(b, 0, k_taken, 1)
                if first and at == 1:
                    wT_of(3)
                    gateT_of(bank[5])
                if at == PE_AT["k1"]:
                    k_of(b, 1, v_taken, value(b, 2, 1))
                if not last and at == PE_AT["xnT0"]:
                    xnT_of(b + 1, 0, v_taken, value(b, 2, 1))
                if not last and at == PE_AT["xnT1"]:
                    xnT_of(b + 1, 1, k_taken, value(b, 2, 2))
                for g in range(2):
                    if not last and at == PE_AT[f"q{g}"]:
                        q_of(b + 1, g)
                for m in range(2):
                    if not first and at == PE_AT[f"project{m}"]:
                        if last:
                            project(b - 1, m, (v_taken, k_taken)[m], value(b, 2, m + 1))
                        else:
                            project(b - 1, m, q_taken, value(b + 1, 2, m + 1))
                if not last and at == PE_AT["ctxT0"]:
                    if first:
                        ctxT_of(b + 1, 0, ps_misc[0], q_taken, value(b + 1, 2, 1))
                    else:
                        ctxT_of(b + 1, 0, ps_misc[0], x1_ready, value(b - 1, 2, 1))
                if at == PE_AT["v1"]:
                    if first:
                        v_of(b, 1, q_taken, value(b + 1, 2, 2))
                    else:
                        v_of(b, 1, x1_ready, value(b - 1, 2, 2))
                if not last and at == PE_AT["ctxT1"]:
                    ctxT_of(b + 1, 1, ps_misc[0], ctxT_taken, value(b + 1, 2, 1))
                if not first and at == PE_AT["x1nT0"]:
                    x1nT_of(b - 1, 0, v_taken, value(b, 2, 2))
                if not first and at == PE_AT["x1nT1"]:
                    if last:
                        x1nT_of(b - 1, 1, x1_ready, value(b - 1, 2, 1))
                    else:
                        x1nT_of(b - 1, 1, ctxT_taken, value(b + 1, 2, 2))
                if not last and at == PE_AT["k0"]:
                    if first:
                        k_of(b + 1, 0, ctxT_taken, value(b + 1, 2, 2))
                    else:
                        k_of(b + 1, 0, x1nT_taken, value(b - 1, 2, 2))
                if not first and at == PE_AT["route"]:
                    route(b - 1)
                if not first and at == PE_AT["count"]:
                    count(b - 1)
                if not last and at == PE_AT["v0"]:
                    v_of(b + 1, 0, k_taken, value(b + 1, 2, 1))
                if last and at == UNITS + 0.5:
                    project(b, 0, x1nT_taken, value(b - 1, 2, 2))

            def body(b, first, last):
                for i in range(UNITS + (AV_LAG if last else 0)):
                    if i < UNITS:
                        scores(b, i)
                    rest(i, b, first, last)
                    if first and i == PT_LAG + 1:
                        pe.wait_ge(wT_taken[3], 1)
                    if (i >= PT_LAG or not first) and i - PT_LAG < UNITS:
                        probsT_of(b, i - PT_LAG)
                    if first and i == AV_LAG + 4:
                        pe.wait_ge(wT_taken[4], 1)
                    if i >= AV_LAG or not first:
                        attend(b, i - AV_LAG)
                    rest(i + 0.5, b, first, last)

            def gateT_of(ps):
                pe.wait_ge(w_in[4], 16)
                for k in range(KD):
                    last = pe.transpose(ps[:, k * E:(k + 1) * E], gate_raw[:, k * P:(k + 1) * P], ident[0:E, 0:E])
                last.then_inc(wT_ready, 1)

            pe.wait_ge(consts_ready, 1)
            wT_of(0)
            wT_of(1)
            for k in range(KD):
                xnT_of(0, k)
            for k in range(KD):
                ctxT_of(0, k, bank[4 + k])
            pe.wait_ge(wT_taken[0], 1)
            q_of(0, 0)
            wT_of(2)
            pe.wait_ge(wT_taken[1], 1)
            k_of(0, 0, q_taken, 1)
            q_of(0, 1)
            pe.wait_ge(pads_ready, 2)
            body(0, True, False)
            with pe.Fori(1, B - 1) as b:
                body(b, False, False)
            body(B - 1, False, True)
            project(B - 1, 1, counts_taken, B - 1)
            pe.wait_ge(scores_taken, B * UNITS)
            pe.wait_ge(probsT_taken[0], B * UNITS // 2)
            for m in range(2):
                x1nT_of(B - 1, m, None, 0)
            route(B - 1)
            pe.wait_ge(x1_ready, 2 * B)
            count(B - 1)

            def xdT_of(e, i, first):
                pe.wait_ge(rows_in[i], loaded(e, i))
                if not first:
                    pe.wait_ge(xdT_taken, e)
                for k in range(KD):
                    for s in range(2):
                        last = pe.transpose(ps_xdT[:, k * CAP + s * SR:k * CAP + (s + 1) * SR],
                                            q_rows[i][:, s, k * P:(k + 1) * P], ident[0:SR, 0:SR])
                last.then_inc(xdT_ready, 1)

            def loaded(e, i):
                return 8 * (e - i) + 16

            def first_product(e, i, m, first):
                if m == 0:
                    pe.wait_ge(w1_in[i], loaded(e, i))
                    pe.wait_ge(xdT_taken, e + 1)
                if not first:
                    pe.wait_ge(gelu_done, 3 * e + m - 2)
                for c, f in enumerate(M_BANKS[m]):
                    for k in range(KD):
                        last = pe.matmul(ps_hidden[m][:, c * CAP:(c + 1) * CAP], w1_sb[i][:, k, f * P:(f + 1) * P],
                                         xdT[i][:, k], start=(k == 0), stop=(k == KD - 1))
                last.then_inc(hidden_ready, 1)

            def second_product(e, i, first):
                pe.wait_ge(w2_in[i], loaded(e, i))
                if not first:
                    pe.wait_ge(yT_taken, e)
                for d in range(KD):
                    for k in range(KF):
                        if d == 0 and k in (0, 3, 6):
                            pe.wait_ge(gelu_done, 3 * e + k // 3 + 1)
                        last = pe.matmul(ps_y[:, d * CAP:(d + 1) * CAP], w2_sb[i][:, k, d * P:(d + 1) * P],
                                         hidden[:, k], start=(k == 0), stop=(k == KF - 1))
                last.then_inc(y_ready, 1)

            def yrows_of(e, first):
                pe.wait_ge(yT_taken, e + 1)
                if not first:
                    pe.wait_ge(yrows_taken, e)
                for s in range(2):
                    for d in range(KD):
                        last = pe.transpose(ps_rows[0:SR, s * D + d * P:s * D + (d + 1) * P],
                                            yT[:, d, s * SR:(s + 1) * SR], ident[:])
                last.then_inc(yrows_ready, 1)

            def expert(e, i, before_it, after_it, first, second):
                first_product(e, i, 0, first)
                if before_it:
                    yrows_of(e - 1, second)
                first_product(e, i, 1, first)
                if after_it:
                    xdT_of(e + 1, 1 - i, False)
                first_product(e, i, 2, first)
                second_product(e, i, first)

            pe.wait_ge(scores_taken, B * UNITS)
            pe.wait_ge(att_taken, B * CHUNKS)
            for i in range(2):
                pe.wait_ge(probsT_taken[i], B * UNITS // 2)
            xdT_of(0, 0, True)
            expert(0, 0, False, True, True, False)
            expert(1, 1, True, True, False, True)
            with pe.Fori(1, E // 2 - 1) as turn:
                expert(2 * turn, 0, True, True, False, False)
                expert(2 * turn + 1, 1, True, True, False, False)
            expert(E - 2, 0, True, True, False, False)
            expert(E - 1, 1, True, False, False, False)
            yrows_of(E - 1, False)


_INS = ['x', 'ctx_1024', 'mask_BxS2_bf1', 'g_xattn', 'g_ffn', 'L0_xattn_W_q', 'L0_xattn_b_q', 'L0_xattn_W_k',
        'L0_xattn_b_k', 'L0_xattn_W_v', 'L0_xattn_b_v', 'L0_xattn_W_o', 'L0_xattn_b_o', 'L0_ffn_gate_w',
        'L0_ffn_w1', 'L0_ffn_w2']
_OUTS = [((4, 512, 256), 'float32')]


def kernel(**inputs):
    import numpy as _np
    import concourse.bacc as _bacc
    from concourse import mybir as _mybir
    from concourse.bass_utils import run_bass_kernel_spmd as _run

    nc = _bacc.Bacc("TRN2", target_bir_lowering=False, num_devices=1)
    arrays, args = {}, []
    for name in _INS:
        a = _np.ascontiguousarray(inputs[name])
        if a.dtype.kind == "b":
            a = a.view(_np.uint8)
        arrays[f"in_{name}_dram"] = a
        args.append(nc.dram_tensor(f"in_{name}_dram", a.shape, _mybir.dt.from_np(a.dtype), kind="ExternalInput").ap())
    for i, (shape, dtype) in enumerate(_OUTS):
        dt = _mybir.dt.from_np(_np.dtype(dtype))
        args.append(nc.dram_tensor(f"out_{i}_dram", shape, dt, kind="ExternalOutput").ap())
    flamingo_kernel(nc, *args)
    r = _run(nc, [arrays], core_ids=[0])
    got = tuple(r.results[0][f"out_{i}_dram"] for i in range(len(_OUTS)))
    return got[0]
```
